# Optimizing a Trainium2 kernel written in Bass

```python
import numpy as np
import jax
import jax.numpy as jnp

def _softmax(x, axis=-1):
    return jax.nn.softmax(x, axis=axis)

def _gelu(x):
    return jax.nn.gelu(x, approximate=True)

def _silu(x):
    return jax.nn.silu(x)

def _sigmoid(x):
    return jax.nn.sigmoid(x)

def _layernorm(x, axis=-1, eps=1e-05):
    m = jnp.mean(x, axis=axis, keepdims=True)
    v = jnp.var(x, axis=axis, keepdims=True)
    return (x - m) / jnp.sqrt(v + eps)

def _scatter_add(tgt, idx, src, axis=0):
    return tgt.at[idx].add(src)

def _segment_sum(src, seg, n):
    return jax.ops.segment_sum(src, seg, n)
kernel_name = 'mk_seq_preln_d1_jaxref_r8_ef38d2'

def setup_inputs(seed: int=0):
    np.random.seed(seed)
    _w = jnp.asarray

    def _L0_attn_setup():
        import jax, jax.numpy as jnp
        import numpy as np
        HEADS = 16
        HEAD_DIM = 64
        EMB = 128
        B, S = (4, 256)
        SCALE = 1.0 / 8.0
        MASK_PENALTY = -50.0
        key = jax.random.key(seed)
        ks = jax.random.split(key, 5)
        x = jax.random.normal(ks[0], (B, S, EMB), dtype=jnp.float32)
        Wq = jax.random.normal(ks[1], (EMB, HEADS * HEAD_DIM), dtype=jnp.float32) * 0.02
        Wk = jax.random.normal(ks[2], (EMB, HEADS * HEAD_DIM), dtype=jnp.float32) * 0.02
        Wv = jax.random.normal(ks[3], (EMB, HEADS * HEAD_DIM), dtype=jnp.float32) * 0.02
        Wr = jax.random.normal(ks[4], (HEADS * HEAD_DIM, EMB), dtype=jnp.float32) * 0.02
        return {'x': x, 'Wq': Wq, 'Wk': Wk, 'Wv': Wv, 'Wr': Wr}
    _L0_attn_in = _L0_attn_setup()

    def _L0_ffn_setup():
        import jax, jax.numpy as jnp
        import numpy as np
        DIM = 128
        DEPTH = 6
        HEADS = 16
        DIM_HEAD = 64
        WINDOW = 32
        INNER = HEADS * DIM_HEAD
        DIM_INNER = int(DIM * 4 * 2 / 3)
        QK_SCALE = 8.0

        def shift_tokens(t):
            a, s = jnp.split(t, 2, -1)
            s = jnp.pad(s, ((0, 0), (1, 0), (0, 0)))[:, :-1]
            return jnp.concatenate([a, s], -1)

        def l2norm(t):
            return t / jnp.maximum(jnp.linalg.norm(t, axis=-1, keepdims=True), 1e-12)

        def rotate_half(x):
            x1, x2 = jnp.split(x, 2, -1)
            return jnp.concatenate([-x2, x1], -1)

        def rotary_tables(n):
            half = jnp.arange(0, DIM_HEAD, 2, dtype=jnp.float32)
            inv_freq = 1.0 / 10000.0 ** (half / DIM_HEAD)
            t = jnp.arange(n, dtype=jnp.float32)
            freqs = t[:, None] * inv_freq[None, :]
            freqs = jnp.concatenate([freqs, freqs], -1)
            base_scale = (half + 0.4 * DIM_HEAD) / (1.4 * DIM_HEAD)
            power = (t - n // 2) / (WINDOW // 2)
            scale = base_scale[None, :] ** power[:, None]
            scale = jnp.concatenate([scale, scale], -1)
            return (freqs, scale)

        def local_attention(q, k, v):
            b, h, n, d = q.shape
            w = WINDOW
            nw = n // w
            bq = q.reshape(b, h, nw, w, d)
            bk = k.reshape(b, h, nw, w, d)
            bv = v.reshape(b, h, nw, w, d)

            def look(t):
                p = jnp.pad(t, ((0, 0), (0, 0), (1, 0), (0, 0), (0, 0)))
                return jnp.concatenate([p[:, :, :nw], p[:, :, 1:]], axis=3)
            bk2, bv2 = (look(bk), look(bv))
            seq = jnp.arange(n).reshape(nw, w)
            seq_p = jnp.pad(seq, ((1, 0), (0, 0)), constant_values=-1)
            jt = jnp.concatenate([seq_p[:nw], seq_p[1:]], axis=1)
            it = seq[:, :, None]
            jb = jt[:, None, :]
            mask = (it < jb) | (it > jb + w) | (jb == -1)
            sim = jnp.einsum('bhwie,bhwje->bhwij', bq, bk2) * QK_SCALE
            sim = jnp.where(mask, -jnp.finfo(sim.dtype).max, sim)
            attn = jax.nn.softmax(sim, -1)
            out = jnp.einsum('bhwij,bhwje->bhwie', attn, bv2)
            return out.reshape(b, h, n, d)

        def attn_layer(x, Wqkv, qs, ksc, Wo):
            b, n, _ = x.shape
            qkv = x @ Wqkv
            q, k, v = jnp.split(qkv, 3, -1)
            sh = lambda t: t.reshape(b, n, HEADS, DIM_HEAD).transpose(0, 2, 1, 3)
            q, k, v = (sh(q), sh(k), sh(v))
            q = l2norm(q) * qs
            k = l2norm(k) * ksc
            freqs, scale = rotary_tables(n)
            cos, sin = (jnp.cos(freqs), jnp.sin(freqs))
            q = q * cos * scale + rotate_half(q) * sin * scale
            inv = 1.0 / scale
            k = k * cos * inv + rotate_half(k) * sin * inv
            out = local_attention(q, k, v)
            out = out.transpose(0, 2, 1, 3).reshape(b, n, INNER)
            return out @ Wo

        def ffn_layer(x, g, bln, W1, b1, W2, b2):
            mu = x.mean(-1, keepdims=True)
            var = ((x - mu) ** 2).mean(-1, keepdims=True)
            xn = (x - mu) / jnp.sqrt(var + 1e-05) * g + bln
            hg = xn @ W1 + b1
            a, gate = jnp.split(hg, 2, -1)
            return a * jax.nn.gelu(gate, approximate=False) @ W2 + b2
        key = jax.random.key(seed)
        ks = jax.random.split(key, 8)
        B, N = (2, 256)
        init = lambda k, shape: jax.random.normal(k, shape, jnp.float32) * 0.02
        return {'x': jax.random.normal(ks[0], (B, N, DIM), jnp.float32), 'Wqkv': init(ks[1], (DEPTH, DIM, 3 * INNER)), 'q_scale': jnp.ones((DEPTH, DIM_HEAD), jnp.float32), 'k_scale': jnp.ones((DEPTH, DIM_HEAD), jnp.float32), 'Wo': init(ks[2], (DEPTH, INNER, DIM)), 'ln_g': jnp.ones((DEPTH, DIM), jnp.float32), 'ln_b': jnp.zeros((DEPTH, DIM), jnp.float32), 'W1': init(ks[3], (DEPTH, DIM, 2 * DIM_INNER)), 'b1': jnp.zeros((DEPTH, 2 * DIM_INNER), jnp.float32), 'W2': init(ks[4], (DEPTH, DIM_INNER, DIM)), 'b2': jnp.zeros((DEPTH, DIM), jnp.float32)}
    _L0_ffn_in = _L0_ffn_setup()
    _d = {'L0_attn_x': _L0_attn_in['x'], 'L0_attn_Wq': _L0_attn_in['Wq'], 'L0_attn_Wk': _L0_attn_in['Wk'], 'L0_attn_Wv': _L0_attn_in['Wv'], 'L0_attn_Wr': _L0_attn_in['Wr'], 'L0_ffn_Wqkv': _L0_ffn_in['Wqkv'], 'L0_ffn_q_scale': _L0_ffn_in['q_scale'], 'L0_ffn_k_scale': _L0_ffn_in['k_scale'], 'L0_ffn_Wo': _L0_ffn_in['Wo'], 'L0_ffn_ln_g': _L0_ffn_in['ln_g'], 'L0_ffn_ln_b': _L0_ffn_in['ln_b'], 'L0_ffn_W1': _L0_ffn_in['W1'], 'L0_ffn_b1': _L0_ffn_in['b1'], 'L0_ffn_W2': _L0_ffn_in['W2'], 'L0_ffn_b2': _L0_ffn_in['b2']}
    _x0 = _d['L0_attn_x']
    _d['L0_attn_x'] = jax.random.normal(jax.random.fold_in(jax.random.key(seed), 1), (4, 512, 128), dtype=_x0.dtype)
    del _x0
    return _d

def reference(L0_attn_x, L0_attn_Wq, L0_attn_Wk, L0_attn_Wv, L0_attn_Wr, L0_ffn_Wqkv, L0_ffn_q_scale, L0_ffn_k_scale, L0_ffn_Wo, L0_ffn_ln_g, L0_ffn_ln_b, L0_ffn_W1, L0_ffn_b1, L0_ffn_W2, L0_ffn_b2):

    def _L0_attn_ref(x, Wq, Wk, Wv, Wr):
        import jax, jax.numpy as jnp
        import numpy as np
        HEADS = 16
        HEAD_DIM = 64
        EMB = 128
        B, S = (4, 256)
        SCALE = 1.0 / 8.0
        MASK_PENALTY = -50.0
        b, s, _ = x.shape
        q = (x @ Wq).reshape(b, s, HEADS, HEAD_DIM)
        k = (x @ Wk).reshape(b, s, HEADS, HEAD_DIM)
        v = (x @ Wv).reshape(b, s, HEADS, HEAD_DIM)
        scores = SCALE * jnp.einsum('bqhd,bkhd->bhqk', q, k)
        causal = jnp.triu(jnp.ones((s, s), dtype=x.dtype), k=1)
        scores = scores + MASK_PENALTY * causal
        attn = jax.nn.softmax(scores, axis=-1)
        out = jnp.einsum('bhqk,bkhd->bqhd', attn, v).reshape(b, s, HEADS * HEAD_DIM)
        return out @ Wr

    def _L0_ffn_ref(x, Wqkv, q_scale, k_scale, Wo, ln_g, ln_b, W1, b1, W2, b2):
        import jax, jax.numpy as jnp
        import numpy as np
        DIM = 128
        DEPTH = 6
        HEADS = 16
        DIM_HEAD = 64
        WINDOW = 32
        INNER = HEADS * DIM_HEAD
        DIM_INNER = int(DIM * 4 * 2 / 3)
        QK_SCALE = 8.0

        def shift_tokens(t):
            a, s = jnp.split(t, 2, -1)
            s = jnp.pad(s, ((0, 0), (1, 0), (0, 0)))[:, :-1]
            return jnp.concatenate([a, s], -1)

        def l2norm(t):
            return t / jnp.maximum(jnp.linalg.norm(t, axis=-1, keepdims=True), 1e-12)

        def rotate_half(x):
            x1, x2 = jnp.split(x, 2, -1)
            return jnp.concatenate([-x2, x1], -1)

        def rotary_tables(n):
            half = jnp.arange(0, DIM_HEAD, 2, dtype=jnp.float32)
            inv_freq = 1.0 / 10000.0 ** (half / DIM_HEAD)
            t = jnp.arange(n, dtype=jnp.float32)
            freqs = t[:, None] * inv_freq[None, :]
            freqs = jnp.concatenate([freqs, freqs], -1)
            base_scale = (half + 0.4 * DIM_HEAD) / (1.4 * DIM_HEAD)
            power = (t - n // 2) / (WINDOW // 2)
            scale = base_scale[None, :] ** power[:, None]
            scale = jnp.concatenate([scale, scale], -1)
            return (freqs, scale)

        def local_attention(q, k, v):
            b, h, n, d = q.shape
            w = WINDOW
            nw = n // w
            bq = q.reshape(b, h, nw, w, d)
            bk = k.reshape(b, h, nw, w, d)
            bv = v.reshape(b, h, nw, w, d)

            def look(t):
                p = jnp.pad(t, ((0, 0), (0, 0), (1, 0), (0, 0), (0, 0)))
                return jnp.concatenate([p[:, :, :nw], p[:, :, 1:]], axis=3)
            bk2, bv2 = (look(bk), look(bv))
            seq = jnp.arange(n).reshape(nw, w)
            seq_p = jnp.pad(seq, ((1, 0), (0, 0)), constant_values=-1)
            jt = jnp.concatenate([seq_p[:nw], seq_p[1:]], axis=1)
            it = seq[:, :, None]
            jb = jt[:, None, :]
            mask = (it < jb) | (it > jb + w) | (jb == -1)
            sim = jnp.einsum('bhwie,bhwje->bhwij', bq, bk2) * QK_SCALE
            sim = jnp.where(mask, -jnp.finfo(sim.dtype).max, sim)
            attn = jax.nn.softmax(sim, -1)
            out = jnp.einsum('bhwij,bhwje->bhwie', attn, bv2)
            return out.reshape(b, h, n, d)

        def attn_layer(x, Wqkv, qs, ksc, Wo):
            b, n, _ = x.shape
            qkv = x @ Wqkv
            q, k, v = jnp.split(qkv, 3, -1)
            sh = lambda t: t.reshape(b, n, HEADS, DIM_HEAD).transpose(0, 2, 1, 3)
            q, k, v = (sh(q), sh(k), sh(v))
            q = l2norm(q) * qs
            k = l2norm(k) * ksc
            freqs, scale = rotary_tables(n)
            cos, sin = (jnp.cos(freqs), jnp.sin(freqs))
            q = q * cos * scale + rotate_half(q) * sin * scale
            inv = 1.0 / scale
            k = k * cos * inv + rotate_half(k) * sin * inv
            out = local_attention(q, k, v)
            out = out.transpose(0, 2, 1, 3).reshape(b, n, INNER)
            return out @ Wo

        def ffn_layer(x, g, bln, W1, b1, W2, b2):
            mu = x.mean(-1, keepdims=True)
            var = ((x - mu) ** 2).mean(-1, keepdims=True)
            xn = (x - mu) / jnp.sqrt(var + 1e-05) * g + bln
            hg = xn @ W1 + b1
            a, gate = jnp.split(hg, 2, -1)
            return a * jax.nn.gelu(gate, approximate=False) @ W2 + b2
        for i in range(DEPTH):
            x = attn_layer(shift_tokens(x), Wqkv[i], q_scale[i], k_scale[i], Wo[i]) + x
            x = ffn_layer(shift_tokens(x), ln_g[i], ln_b[i], W1[i], b1[i], W2[i], b2[i]) + x
        return x
    x = L0_attn_x
    x = x + _L0_attn_ref(_layernorm(x, axis=-1), L0_attn_Wq, L0_attn_Wk, L0_attn_Wv, L0_attn_Wr)
    x = x + _L0_ffn_ref(_layernorm(x, axis=-1), L0_ffn_Wqkv, L0_ffn_q_scale, L0_ffn_k_scale, L0_ffn_Wo, L0_ffn_ln_g, L0_ffn_ln_b, L0_ffn_W1, L0_ffn_b1, L0_ffn_W2, L0_ffn_b2)
    return x

_drawn_inputs = setup_inputs


def setup_inputs(seed=0):
    import zlib

    import numpy as np

    out = dict(_drawn_inputs(seed))
    spreads = {'L0_ffn_q_scale': (1.0, 0.6),
     'L0_ffn_k_scale': (1.0, 0.6),
     'L0_ffn_ln_g': (1.0, 0.6),
     'L0_ffn_ln_b': (0.0, 0.8),
     'L0_ffn_b1': (0.0, 0.8),
     'L0_ffn_b2': (0.0, 0.1)}
    factors = {'L0_attn_Wq': 8.0,
     'L0_attn_Wk': 8.0,
     'L0_attn_Wv': 3.459,
     'L0_attn_Wr': 3.387,
     'L0_ffn_W1': 3.641,
     'L0_ffn_W2': 3.573}
    for name, (base, spread) in spreads.items():
        noise = np.random.default_rng([zlib.crc32(name.encode()), seed]).standard_normal(out[name].shape)
        drawn = base * np.exp(spread * noise) if base else spread * noise
        out[name] = jnp.asarray(drawn.astype(out[name].dtype))
    for name, factor in factors.items():
        out[name] = (out[name] * factor).astype(out[name].dtype)
    return out
```

```python
from contextlib import ExitStack

import concourse.bass as bass
from concourse import mybir

F32 = mybir.dt.float32
BF16 = mybir.dt.bfloat16
ALU = mybir.AluOpType
ACT = mybir.ActivationFunctionType
AX = mybir.AxisListType

P = 128
E = 128
HEADS = 16
DH = 64
INNER = HEADS * DH
PAIRS = HEADS // 2
BATCH = 4
SEQ = 512
TPB = SEQ // P
TILES = BATCH * TPB
DEPTH = 6
WIN = 32
GRP = 2 * WIN
SPAN = GRP + WIN
HG = 4
NHG = HEADS // HG
FF = int(E * 4 * 2 / 3)
FFC = [(c, min(P, FF - c)) for c in range(0, FF, P)]
STEPS = DEPTH * BATCH
PENALTY = -50.0
FORBID = -1e25
SCALE = 0.125
QK_SCALE = 8.0
LN_EPS = 1e-5
NORM2_EPS = 1e-24


class Sig:

    def __init__(self, nc, ctx, name, per, owner, lag=1):
        self.sem = ctx.enter_context(nc.semaphore(name))
        self.per, self.owner, self.lag = per, owner, lag

    def start(self, engine):
        engine.sem_inc(self.sem, self.lag * self.per)

    def inc(self, ins):
        ins.then_inc(self.sem, 1)

    def wait(self, engine, unit, event=None):
        n = self.per - 1 if event is None else event
        engine.wait_ge(self.sem, (unit + self.lag) * self.per + n + 1)


def engines_run(nc, sigs, program):
    with nc.Block() as block:
        for name, deco in (("pe", block.tensor), ("act", block.scalar), ("dve", block.vector),
                           ("pool", block.gpsimd), ("sp", block.sync)):
            def body(eng, name=name):
                for s in sigs:
                    if s.owner == name:
                        s.start(eng)
                program(name, eng)
            deco(body)


def build(nc, x, wq, wk, wv, wr, wqkv, qscale, kscale, wo, lng, lnb, w1, b1, w2, b2, rot, out):
    with ExitStack() as keep:
        def sb(name, shape, dt=F32, ctx=keep):
            return ctx.enter_context(nc.sbuf_tensor(name, shape, dt))

        bank = [keep.enter_context(nc.psum_tensor(f"bank{i}", [P, 512], F32)) for i in range(8)]
        X = sb("X", [P, TILES, E])
        XM = sb("XM", [P, TILES, E])
        ident = sb("ident", [P, P])
        s_c = keep.enter_context(nc.semaphore("s_const"))

        passed = {}

        def settle(eng):
            k = str(eng.engine)
            if k not in passed:
                passed[k] = keep.enter_context(nc.semaphore(f"passed{len(passed)}"))
            eng.sem_inc(passed[k], 1)

        identb = sb("identb", [P, P], BF16)
        stats = sb("stats", [P, TPB, 6])
        mv = sb("mv", [P, TPB, 2])
        veps = sb("veps", [P, TPB])
        rstd = sb("rstd", [P, TPB])
        mhalf = sb("mhalf", [P, 64])

        def in_dma(engine, sem, dst, src):
            engine.dma_start(dst, src).then_inc(sem, 16)

        x_t = x.rearrange("b (t p) e -> p (b t) e", p=P)
        out_t = out.rearrange("b (t p) e -> p (b t) e", p=P)

        with ExitStack() as ctx:
            def sbl(name, shape, dt=F32):
                return sb(name, shape, dt, ctx)

            W0 = sbl("W0", [P, 3, INNER])
            WR = sbl("WR", [P, PAIRS, E])
            XNT = sbl("XNT", [P, BATCH * SEQ])
            XN0 = sbl("XN0", [P, TPB, E])
            WP = [sbl(f"WP{i}", [P, 3, P]) for i in range(2)]
            XNS = [sbl(f"XNS{i}", [P, SEQ]) for i in range(2)]
            QT = [sbl(f"QT{i}", [P, SEQ]) for i in range(2)]
            KZ = [sbl(f"KZ{i}", [P, 2, SEQ]) for i in range(2)]
            V = [sbl(f"V{i}", [P, TPB, P]) for i in range(2)]
            PR = [sbl(f"PR{i}", [P, SEQ]) for i in range(2)]
            PTS = [[sbl(f"PTS{i}{e}", [P, TPB, SEQ]) for e in range(2)] for i in range(2)]
            OT = sbl("OT", [P, SEQ])
            NM = sbl("NM", [P, 8])
            RS = sbl("RS", [P, 8])
            RI = sbl("RI", [P, 8])
            causal = sbl("causal", [P, SEQ], BF16)

            s_in = ctx.enter_context(nc.semaphore("s_x"))
            s_w0 = ctx.enter_context(nc.semaphore("s_w0"))
            lnst = Sig(nc, ctx, "lnst", 5, "dve")
            lnve = Sig(nc, ctx, "lnve", 1, "dve")
            lnrs = Sig(nc, ctx, "lnrs", 1, "pool")
            lnxn = Sig(nc, ctx, "lnxn", 4, "dve")
            lntr = Sig(nc, ctx, "lntr", 1, "pe")
            lnev = Sig(nc, ctx, "lnev", 1, "act")

            def ln_program(name, eng):
                if name == "sp":
                    for i in range(2):
                        in_dma(eng, s_in, X[:, 8 * i:8 * i + 8, :], x_t[:, 8 * i:8 * i + 8, :])
                    for i, w in enumerate((wq, wk, wv)):
                        in_dma(eng, s_w0, W0[:, i, :], w)
                    in_dma(eng, s_w0, WR[:, :, :], wr.rearrange("(c p) e -> p c e", p=P))
                    eng.wait_ge(s_w0, 64)
                if name == "pool":
                    eng.memset(ident[:, :], 0.0).then_inc(s_c, 1)
                    eng.memset(identb[:, :], 0.0).then_inc(s_c, 1)
                    eng.memset(causal[:, :], 0.0).then_inc(s_c, 1)
                    eng.memset(mhalf[:, :], -0.5).then_inc(s_c, 1)
                    for i in range(2):
                        eng.memset(KZ[i][:, :, :], 0.0).then_inc(s_c, 1)
                    eng.wait_ge(s_c, 6)
                    for m in (ident, identb):
                        eng.affine_select(out=m[:, :], in_=m[:, :], compare_op=ALU.not_equal, fill=1.0,
                                          base=0, pattern=[[-1, P]], channel_multiplier=1).then_inc(s_c, 1)
                    eng.affine_select(out=causal[:, :], in_=causal[:, :], compare_op=ALU.is_ge,
                                      fill=PENALTY, base=0, pattern=[[-1, SEQ]],
                                      channel_multiplier=1).then_inc(s_c, 1)
                if name == "sp":
                    return
                with eng.Fori(0, BATCH) as b:
                    if name == "dve":
                        eng.wait_ge(s_in, 32)
                        for t in range(TPB):
                            lnst.inc(eng.bn_stats(stats[:, t, :], X[:, b * TPB + t, :]))
                        for t in range(TPB):
                            lnst.wait(eng, b, t)
                            settle(eng)
                            i = eng.bn_aggr(mv[:, t, :], stats[:, t, :])
                        lnst.inc(i)
                        lnst.wait(eng, b)
                        lnrs.wait(eng, b - 1)
                        lnve.inc(eng.tensor_scalar(veps[:, :], mv[:, :, 1], LN_EPS, None, ALU.add))
                        lnrs.wait(eng, b)
                        lntr.wait(eng, b - 1)
                        for t in range(TPB):
                            lnxn.inc(eng.tensor_scalar(XN0[:, t, :], X[:, b * TPB + t, :], mv[:, t, 0:1],
                                                       rstd[:, t:t + 1], ALU.subtract, ALU.mult))
                    if name == "pool":
                        eng.wait_ge(s_c, 9)
                        lnve.wait(eng, b)
                        lnrs.inc(eng.tensor_tensor(rstd[:, :], veps[:, :], mhalf[:, 0:TPB], ALU.pow))
                    if name == "pe":
                        eng.wait_ge(s_c, 9)
                        lnxn.wait(eng, b)
                        lnev.wait(eng, b - 1)
                        for t in range(TPB):
                            i = eng.transpose(bank[7][:, t * P:(t + 1) * P], XN0[:, t, :], ident[:, :])
                        lntr.inc(i)
                    if name == "act":
                        lntr.wait(eng, b)
                        lnev.inc(eng.activation(XNT[:, bass.ds(b * SEQ, SEQ)], bank[7][:, :], ACT.Copy))

            engines_run(nc, (lnst, lnve, lnrs, lnxn, lntr, lnev), ln_program)

            NJ = 2 * TPB
            wps = Sig(nc, ctx, "wps", 2, "pool")
            pj = Sig(nc, ctx, "pj", 3, "pe")
            pja = Sig(nc, ctx, "pja", 3, "act")
            pjd = Sig(nc, ctx, "pjd", 1, "dve")
            sc = Sig(nc, ctx, "sc", NJ, "pe", 2)
            nm = Sig(nc, ctx, "nm", NJ, "dve")
            ex = Sig(nc, ctx, "ex", NJ, "act")
            ri = Sig(nc, ctx, "ri", NJ, "dve")
            pn = Sig(nc, ctx, "pn", NJ, "pool")
            pt = Sig(nc, ctx, "pt", NJ, "pe")
            pe = Sig(nc, ctx, "ptc", NJ, "dve")
            av = Sig(nc, ctx, "av", 1, "pe", 2)
            ov = Sig(nc, ctx, "ov", 1, "act")
            yy = Sig(nc, ctx, "yy", 1, "pe")
            xa = Sig(nc, ctx, "xa", 1, "dve")
            sigs0 = (wps, pj, pja, pjd, sc, nm, ex, ri, pn, pt, pe, av, ov, yy, xa)

            def stage(name, eng, u, par):
                if name == "pool":
                    pj.wait(eng, u - 1)
                    w = eng.tensor_copy(WP[par][:, :, :], W0[:, :, bass.ds((u % PAIRS) * P, P)])
                    wps.inc(w)
                    wps.inc(eng.tensor_copy(XNS[par][:, :], XNT[:, bass.ds((u // PAIRS) * SEQ, SEQ)]))

            def project(name, eng, u, par, c):
                pb = bank[c % 2]
                if name == "pe":
                    wps.wait(eng, u)
                    if c == 0:
                        pja.wait(eng, u - 1, 2)
                        eng.matmul(pb[:, :], WP[par][:, 0, :], XNS[par][:, :], start=True, stop=True)\
                           .then_inc(pj.sem, 1)
                    if c == 1:
                        pja.wait(eng, u - 1, 1)
                        pjd.wait(eng, u - 1)
                        eng.matmul(pb[:, :], WP[par][:, 1, :], XNS[par][:, :], start=True, stop=True)\
                           .then_inc(pj.sem, 1)
                    if c == 2:
                        pja.wait(eng, u, 0)
                        for t in range(TPB):
                            i = eng.matmul(pb[:, t * P:(t + 1) * P], XNS[par][:, t * P:(t + 1) * P],
                                           WP[par][:, 2, :], start=True, stop=True)
                        pj.inc(i)
                if name == "act":
                    pj.wait(eng, u, c)
                    if c == 0:
                        sc.wait(eng, u - 2)
                        pja.inc(eng.activation(QT[par][:, :], pb[:, :], ACT.Copy))
                    if c == 1:
                        pja.inc(eng.activation(KZ[par][DH:P, 1, :], pb[DH:P, :], ACT.Copy, scale=SCALE))
                    if c == 2:
                        av.wait(eng, u - 2)
                        pja.inc(eng.activation(V[par][:, :, :], pb[:, :].rearrange("p (t d) -> p t d", t=TPB),
                                               ACT.Copy))
                if name == "dve" and c == 1:
                    pj.wait(eng, u, 1)
                    sc.wait(eng, u - 2)
                    pjd.inc(eng.tensor_scalar(KZ[par][0:DH, 0, :], pb[0:DH, :], SCALE, None, ALU.mult))

            def scores(name, eng, u, par, j):
                qt, e = divmod(j, 2)
                sbk = bank[2 + j % 2]
                if name == "pe":
                    pja.wait(eng, u, 1)
                    pjd.wait(eng, u)
                    if j >= 2:
                        ex.wait(eng, u, j - 2)
                    else:
                        ex.wait(eng, u - 1, NJ - 2 + j)
                    eng.matmul(sbk[:, :], QT[par][:, qt * P:(qt + 1) * P], KZ[par][:, e, :],
                               start=True, stop=False, skip_group_check=True)
                    sc.inc(eng.matmul(sbk[:, qt * P:SEQ], identb[:, :], causal[:, 0:SEQ - qt * P],
                                      start=False, stop=True, skip_group_check=True))

            def softmax(name, eng, u, par, j):
                sbk = bank[2 + j % 2]
                if name == "dve":
                    sc.wait(eng, u, j)
                    ex.wait(eng, u - 1, j)
                    nm.inc(eng.tensor_reduce(NM[:, j:j + 1], sbk[:, :], AX.X, ALU.max, negate=True))
                if name == "act":
                    nm.wait(eng, u, j)
                    ri.wait(eng, u - 1, j)
                    if j >= 2:
                        pt.wait(eng, u, j - 2)
                    else:
                        pt.wait(eng, u - 1, NJ - 2 + j)
                    ex.inc(eng.activation(PR[j % 2][:, :], sbk[:, :], ACT.Exp, bias=NM[:, j:j + 1],
                                          accum_out=RS[:, j:j + 1]))

            def normalise(name, eng, u, par, j):
                if name == "dve":
                    ex.wait(eng, u, j)
                    pn.wait(eng, u - 1, j)
                    ri.inc(eng.reciprocal(RI[:, j:j + 1], RS[:, j:j + 1]))
                if name == "pool":
                    ri.wait(eng, u, j)
                    settle(eng)
                    pn.inc(eng.tensor_scalar(PR[j % 2][:, :], PR[j % 2][:, :], RI[:, j:j + 1], None, ALU.mult))

            def transpose_p(name, eng, u, par, j):
                qt, e = divmod(j, 2)
                tb = bank[4 + j % 2]
                if name == "pe":
                    pn.wait(eng, u, j)
                    if j >= 2:
                        pe.wait(eng, u, j - 2)
                    else:
                        pe.wait(eng, u - 1, NJ - 2 + j)
                    for k in range(TPB):
                        i = eng.transpose(tb[:, k * P:(k + 1) * P], PR[j % 2][:, k * P:(k + 1) * P], ident[:, :])
                    pt.inc(i)
                if name == "dve":
                    pt.wait(eng, u, j)
                    av.wait(eng, u - 2)
                    pe.inc(eng.tensor_copy(PTS[par][e][:, :, qt * P:(qt + 1) * P],
                                           tb[:, :].rearrange("p (k q) -> p k q", k=TPB)))

            def times_v(name, eng, u, par):
                if name == "pe":
                    pja.wait(eng, u, 2)
                    pe.wait(eng, u)
                    ov.wait(eng, u - 1)
                    for k in range(TPB):
                        for e in range(2):
                            i = eng.matmul(bank[6][e * DH:(e + 1) * DH, :], V[par][:, k, e * DH:(e + 1) * DH],
                                           PTS[par][e][:, k, :], start=(k == 0), stop=(k == TPB - 1))
                    av.inc(i)
                if name == "act":
                    av.wait(eng, u)
                    yy.wait(eng, u - 1)
                    ov.inc(eng.activation(OT[:, :], bank[6][:, :], ACT.Copy))

            def project_out(name, eng, u, par):
                if name == "pe":
                    ov.wait(eng, u)
                    xa.wait(eng, u - 1)
                    for t in range(TPB):
                        i = eng.matmul(bank[7][:, t * P:(t + 1) * P], OT[:, t * P:(t + 1) * P],
                                       WR[:, u % PAIRS, :], start=True, stop=True)
                    yy.inc(i)
                if name == "dve":
                    yy.wait(eng, u)
                    xa.wait(eng, u - 1)
                    xs = X[:, bass.ds((u // PAIRS) * TPB, TPB), :]
                    xa.inc(eng.tensor_tensor(xs, xs, bank[7][:, :].rearrange("p (t e) -> p t e", t=TPB), ALU.add))

            def pair(name, eng, u, par, nxt=True):
                for j in range(NJ):
                    if j == 0 and nxt:
                        stage(name, eng, u + 1, 1 - par)
                    if j + 2 < NJ:
                        scores(name, eng, u, par, j + 2)
                    elif nxt and j + 2 == NJ:
                        scores(name, eng, u + 1, 1 - par, 0)
                    transpose_p(name, eng, u, par, j)
                    if j + 2 < NJ:
                        softmax(name, eng, u, par, j + 2)
                        normalise(name, eng, u, par, j + 2)
                    elif nxt and j + 2 == NJ:
                        softmax(name, eng, u + 1, 1 - par, 0)
                        normalise(name, eng, u + 1, 1 - par, 0)
                    if nxt and j in (1, 2, 3):
                        project(name, eng, u + 1, 1 - par, j - 1)
                times_v(name, eng, u, par)
                if nxt:
                    scores(name, eng, u + 1, 1 - par, 1)
                    softmax(name, eng, u + 1, 1 - par, 1)
                    normalise(name, eng, u + 1, 1 - par, 1)
                project_out(name, eng, u, par)

            def attn_program(name, eng):
                if name == "sp":
                    return
                stage(name, eng, 0, 0)
                for c in range(3):
                    project(name, eng, 0, 0, c)
                for j in range(2):
                    scores(name, eng, 0, 0, j)
                    softmax(name, eng, 0, 0, j)
                    normalise(name, eng, 0, 0, j)
                last = BATCH * PAIRS // 2 - 1
                with eng.Fori(0, last) as v:
                    for par in range(2):
                        pair(name, eng, 2 * v + par, par)
                pair(name, eng, 2 * last, 0)
                pair(name, eng, 2 * last + 1, 1, nxt=False)

            engines_run(nc, sigs0, attn_program)

        with ExitStack() as ctx:
            def sbl(name, shape, dt=F32):
                return sb(name, shape, dt, ctx)

            WQKV = sbl("WQKV", [P, 2, 3 * INNER])
            WO = sbl("WO", [P, 2, PAIRS, E])
            W1 = sbl("W1", [P, 2, 2 * FF])
            W2 = sbl("W2", [P, 2, len(FFC), E])
            QKS = sbl("QKS", [P, 2, 2, DH])
            B1 = sbl("B1", [P, 2, 2 * FF])
            B2 = sbl("B2", [P, 2, E])
            ROT = sbl("ROT", [P, 4, TPB, DH])
            RT = sbl("RT", [P, 4, TPB, DH])
            band = sbl("band", [P, 2, HG, SPAN], BF16)

            XS = [sbl(f"XS{i}", [P, E]) for i in range(2)]
            XT = sbl("XT", [P, WIN + SEQ + 1])
            QR = sbl("QR", [P, 4, 512])
            SQ = [sbl(f"SQ{i}", [P, 512]) for i in range(2)]
            T2 = [sbl(f"T2{i}", [P, 512]) for i in range(2)]
            TQ = sbl("TQ", [P, 4, 512])
            SS = sbl("SS", [P, 4, 8])
            SM = sbl("SM", [P, 4, 8])
            RN = sbl("RN", [P, 4, 8])
            VG = [sbl(f"VG{i}", [SPAN, 2, INNER]) for i in range(2)]
            QTL = sbl("QTL", [P, PAIRS, P])
            KZL = sbl("KZL", [P, PAIRS, 2, WIN + SEQ])
            PL = [sbl(f"PL{i}", [P, HG, SPAN]) for i in range(2)]
            NML = sbl("NML", [P, HEADS])
            RSL = sbl("RSL", [P, HEADS])
            RIL = sbl("RIL", [P, HEADS])
            PTL = [sbl(f"PTL{i}", [SPAN, HG * P]) for i in range(2)]
            OTL = sbl("OTL", [P, PAIRS, P])
            X2 = sbl("X2", [P, TPB, E])
            X2B = sbl("X2B", [P, TPB, E])
            XT2 = sbl("XT2", [P, SEQ + 1])
            XN = sbl("XN", [P, TPB, E])
            XNT2 = sbl("XNT2", [P, SEQ])
            A1 = [sbl(f"A1{i}", [P, FF]) for i in range(2)]
            G1 = [sbl(f"G1{i}", [P, FF]) for i in range(2)]
            HT = sbl("HT", [P, len(FFC), P])

            s_i = ctx.enter_context(nc.semaphore("s_i"))
            s_k = ctx.enter_context(nc.semaphore("s_k"))
            s_m = ctx.enter_context(nc.semaphore("s_m"))
            s_w = ctx.enter_context(nc.semaphore("s_w"))
            NW = 10

            def sig(name, per, owner, lag=1):
                s = Sig(nc, ctx, "l_" + name, per, owner, lag)
                sigs.append(s)
                return s
            sigs = []
            xs = sig("xs", 1, "pool")
            fx = sig("fx", 1, "pe")
            fxd = sig("fxd", 1, "dve")
            fxa = sig("fxa", 1, "act")
            ch = sig("ch", 8, "pe")
            cv = sig("cv", 8, "act")
            sq = sig("sq", 4, "act")
            ss = sig("ss", 4, "dve")
            sm = sig("sm", 4, "pool")
            rn = sig("rn", 4, "pool")
            t1 = sig("t1", 4, "dve")
            t2 = sig("t2", 4, "pool")
            ad = sig("ad", 4, "dve")
            qn = sig("qn", 4, "pool")
            tr = sig("tr", 4, "pe")
            qe = sig("qe", 2, "act")
            ke0 = sig("ke0", 2, "dve")
            ke1 = sig("ke1", 2, "act")
            scl = sig("scl", NHG, "pe")
            nml = sig("nml", NHG, "dve")
            exl = sig("exl", NHG, "act")
            ril = sig("ril", NHG, "dve")
            pnl = sig("pnl", NHG, "pool")
            ptl = sig("ptl", NHG, "pe")
            pcl = sig("pcl", NHG, "dve")
            avl = sig("avl", NHG, "pe", 2)
            ovl = sig("ovl", 2, "act")
            yl = sig("yl", 1, "pe")
            x2 = sig("x2", 1, "dve", 2)
            x2b = sig("x2b", 1, "pool")
            rtd = sig("rtd", 2, "dve")
            rtp = sig("rtp", 4, "pool")
            g1 = sig("g1", 1, "pe")
            g1d = sig("g1d", 1, "dve")
            g1a = sig("g1a", 1, "act")
            g2 = sig("g2", 1, "pe")
            gst = sig("gst", 5, "dve")
            gve = sig("gve", 1, "dve")
            grs = sig("grs", 1, "pool")
            gxn = sig("gxn", 1, "dve")
            g3 = sig("g3", 1, "pe")
            gxt = sig("gxt", 1, "act")
            hh = sig("hh", 2 * TPB, "pe")
            hb = sig("hb", 2 * TPB, "dve", 2)
            ge = sig("ge", TPB, "act")
            hm = sig("hm", TPB, "pool")
            ht = sig("ht", TPB, "pe")
            he = sig("he", TPB, "act")
            fy = sig("fy", TPB, "pe")
            fin = sig("fin", TPB, "dve", 2)

            def load_layer(eng, l, par_addr, sem):
                def d(dst, src):
                    eng.dma_start(dst, src).then_inc(sem, 16)
                half = 3 * INNER // 2
                for i in range(2):
                    d(WQKV[:, par_addr, i * half:(i + 1) * half], wqkv[l, :, i * half:(i + 1) * half])
                d(WO[:, par_addr, :, :], wo[l, :, :].rearrange("(c p) e -> p c e", p=P))
                d(W1[:, par_addr, :], w1[l, :, :])
                for c, (c0, n) in enumerate(FFC):
                    if c == 0:
                        d(W2[:, par_addr, 0:2, :], w2[l, 0:2 * P, :].rearrange("(c p) e -> p c e", p=P))
                    elif n < P:
                        d(W2[0:n, par_addr, c, :], w2[l, c0:c0 + n, :])
                d(QKS[:, par_addr, 0, :], qscale[l:l + 1, :].to_broadcast([P, DH]))
                d(QKS[:, par_addr, 1, :], kscale[l:l + 1, :].to_broadcast([P, DH]))
                d(B1[:, par_addr, :], b1[l:l + 1, :].to_broadcast([P, 2 * FF]))
                d(B2[:, par_addr, :], b2[l:l + 1, :].to_broadcast([P, E]))

            def ln_gains(name, eng):
                n = 2 * DEPTH
                if name == "pe":
                    eng.wait_ge(s_i, 48)
                    eng.transpose(bank[5][:, 0:n], LGB[:, :], ident[0:n, 0:n]).then_inc(s_g, 1)
                if name == "dve":
                    eng.wait_ge(s_g, 1)
                    eng.tensor_copy(GBA[:, :, :], bank[5][:, 0:n].rearrange("p (k l) -> p k l", k=2))\
                       .then_inc(s_g, 1)
                if name in ("pe", "act"):
                    eng.wait_ge(s_g, 2)

            LGB = sbl("LGB", [2 * DEPTH, E])
            GBA = sbl("GBA", [P, 2, DEPTH])
            s_g = ctx.enter_context(nc.semaphore("s_g"))

            def rotary_tables(name, eng, s, first=False):
                lp = (s // BATCH) % 2
                if name == "dve":
                    if first:
                        eng.wait_ge(s_i, 48)
                    wait_weights(eng, s)
                    t1.wait(eng, s * TPB - 1)
                    for k in range(2):
                        q = QKS[:, lp, k:k + 1, :].to_broadcast([P, TPB, DH])
                        rtd.inc(eng.tensor_tensor(RT[:, 2 * k, :, :], ROT[:, 2 * k, :, :], q, ALU.mult))
                if name == "pool":
                    if first:
                        eng.wait_ge(s_i, 48)
                    wait_weights(eng, s)
                    t2.wait(eng, s * TPB - 1)
                    settle(eng)
                    for k in range(2):
                        for h in range(2):
                            q = QKS[:, lp, k:k + 1, (1 - h) * 32:(2 - h) * 32].to_broadcast([P, TPB, 32])
                            a = slice(h * 32, h * 32 + 32)
                            rtp.inc(eng.tensor_tensor(RT[:, 2 * k + 1, :, a], ROT[:, 2 * k + 1, :, a], q, ALU.mult))

            def wait_weights(eng, s):
                eng.wait_ge(s_w, (s // BATCH + 1) * 16 * NW)

            def front_x(name, eng, s, t):
                g = s * TPB + t
                b = s % BATCH
                if name == "pool":
                    fx.wait(eng, g - 1)
                    fin.wait(eng, s - 2)
                    xs.inc(eng.tensor_copy(XS[t % 2][:, :], X[:, b * TPB + t, :]))
                if name == "pe":
                    xs.wait(eng, g)
                    x2.wait(eng, g - 2)
                    fin.wait(eng, s - 1 if t else s - 2)
                    fx.inc(eng.transpose(bank[7][:, 0:P], XS[t % 2][:, :], ident[:, :]))
                c0 = WIN + t * P
                if name == "dve":
                    fx.wait(eng, g)
                    fxd.inc(eng.tensor_copy(XT[0:DH, c0:c0 + P], bank[7][0:DH, 0:P]))
                if name == "act":
                    fx.wait(eng, g)
                    fxa.inc(eng.activation(XT[DH:P, c0 + 1:c0 + 1 + P], bank[7][DH:P, 0:P], ACT.Copy))

            def front_chunk(name, eng, s, t, c):
                g = s * TPB + t
                lp = (s // BATCH) % 2
                pb = bank[c % 2]
                c0 = WIN + t * P
                if name == "pe":
                    if c == 0:
                        fxd.wait(eng, g)
                        fxa.wait(eng, g)
                        wait_weights(eng, s)
                    if c >= 2:
                        cv.wait(eng, g, c - 2)
                    else:
                        cv.wait(eng, g - 1, 6 + c)
                        hb.wait(eng, s - 1 if t else s - 2)
                    if c < 4:
                        i = eng.matmul(pb[:, :], XT[:, c0:c0 + P], WQKV[:, lp, c * 512:(c + 1) * 512],
                                       start=True, stop=True)
                    else:
                        grp, half = divmod(c - 4, 2)
                        k0 = t * P + grp * GRP
                        w0 = 2 * INNER + half * 512
                        i = eng.matmul(pb[0:SPAN, :], XT[:, k0:k0 + SPAN], WQKV[:, lp, w0:w0 + 512],
                                       start=True, stop=True)
                    ch.inc(i)
                if name == "act":
                    ch.wait(eng, g, c)
                    if c < 4:
                        t1.wait(eng, g - 1, c)
                        t2.wait(eng, g - 1, c)
                        cv.inc(eng.activation(QR[:, c, :], pb[:, :], ACT.Copy))
                        cv.wait(eng, g, c)
                        if c >= 2:
                            ss.wait(eng, g, c - 2)
                        else:
                            ss.wait(eng, g - 1, 2 + c)
                        sq.inc(eng.activation(SQ[c % 2][:, :], QR[:, c, :], ACT.Square))
                    else:
                        grp, half = divmod(c - 4, 2)
                        avl.wait(eng, g - 2)
                        cv.inc(eng.activation(VG[t % 2][:, grp, half * 512:(half + 1) * 512],
                                              pb[0:SPAN, :], ACT.Copy))

            def front_rotary(name, eng, s, t, c):
                g = s * TPB + t
                k = c // 2
                q3 = QR[:, c, :].rearrange("p (h d) -> p h d", d=DH)
                if name == "dve":
                    cv.wait(eng, g, c)
                    qn.wait(eng, g - 1, c)
                    tr.wait(eng, g - 1, c)
                    if c == 0:
                        rtd.wait(eng, s)
                    cos = RT[:, 2 * k, t:t + 1, :].to_broadcast([P, 8, DH])
                    tq = TQ[:, c, :].rearrange("p (h d) -> p h d", d=DH)
                    t1.inc(eng.tensor_tensor(tq, q3, cos, ALU.mult))
                    sq.wait(eng, g, c)
                    sm.wait(eng, g - 1, c)
                    ss.inc(eng.tensor_reduce(SS[:, c, :], SQ[c % 2][:, :].rearrange("p (h d) -> p h d", d=DH),
                                             AX.X, ALU.add))
                    t2.wait(eng, g, c)
                    t1.wait(eng, g, c)
                    ad.inc(eng.tensor_tensor(TQ[:, c, :], TQ[:, c, :], T2[c % 2][:, :], ALU.add))
                if name == "pool":
                    cv.wait(eng, g, c)
                    if c >= 2:
                        ad.wait(eng, g, c - 2)
                    else:
                        ad.wait(eng, g - 1, 2 + c)
                    if c == 0:
                        rtp.wait(eng, s)
                    settle(eng)
                    o3 = T2[c % 2][:, :].rearrange("p (h d) -> p h d", d=DH)
                    for h in range(2):
                        sin = RT[:, 2 * k + 1, t:t + 1, h * 32:h * 32 + 32].to_broadcast([P, 8, 32])
                        i = eng.tensor_tensor(o3[:, :, h * 32:h * 32 + 32],
                                              q3[:, :, (1 - h) * 32:(2 - h) * 32], sin, ALU.mult)
                    t2.inc(i)
                    ss.wait(eng, g, c)
                    settle(eng)
                    sm.inc(eng.tensor_scalar(SM[:, c, :], SS[:, c, :], NORM2_EPS, None, ALU.max))
                    sm.wait(eng, g, c)
                    rn.inc(eng.tensor_tensor(RN[:, c, :], SM[:, c, :], mhalf[:, 0:8], ALU.pow))
                    rn.wait(eng, g, c)
                    ad.wait(eng, g, c)
                    tq = TQ[:, c, :].rearrange("p (h d) -> p h d", d=DH)
                    r = RN[:, c, :].rearrange("p (h a) -> p h a", a=1).to_broadcast([P, 8, DH])
                    qn.inc(eng.tensor_tensor(tq, tq, r, ALU.mult))

            def feature_major(name, eng, s, t, c):
                g = s * TPB + t
                tb = bank[5]
                if name == "pe":
                    qn.wait(eng, g, c)
                    if c == 0:
                        ke0.wait(eng, g - 1)
                        ke1.wait(eng, g - 1)
                        he.wait(eng, s - 1)
                    elif c < 3:
                        qe.wait(eng, g, c - 1)
                    else:
                        ke0.wait(eng, g, 0)
                        ke1.wait(eng, g, 0)
                    for i in range(4):
                        m = eng.transpose(tb[:, i * P:(i + 1) * P], TQ[:, c, i * P:(i + 1) * P], ident[:, :])
                    tr.inc(m)
                v4 = tb[:, :].rearrange("p (i q) -> p i q", i=4)
                if name == "act":
                    tr.wait(eng, g, c)
                    scl.wait(eng, g - 1)
                    if c < 2:
                        qe.inc(eng.activation(QTL[:, 4 * c:4 * c + 4, :], v4, ACT.Copy))
                    else:
                        a = 4 * (c - 2)
                        ke1.inc(eng.activation(KZL[DH:P, a:a + 4, 1, WIN + t * P:WIN + (t + 1) * P],
                                               v4[DH:P, :, :], ACT.Copy))
                if name == "dve" and c >= 2:
                    tr.wait(eng, g, c)
                    scl.wait(eng, g - 1)
                    a = 4 * (c - 2)
                    ke0.inc(eng.tensor_copy(KZL[0:DH, a:a + 4, 0, WIN + t * P:WIN + (t + 1) * P], v4[0:DH, :, :]))

            def local_scores(name, eng, s, t, hg):
                g = s * TPB + t
                sbk = bank[2 + hg % 2]
                n = HG * SPAN
                if name == "pe":
                    if hg == 0:
                        hb.wait(eng, s - 1)
                    if hg % 2 == 0:
                        qe.wait(eng, g, hg // 2)
                        ke0.wait(eng, g, hg // 2)
                        ke1.wait(eng, g, hg // 2)
                    if hg >= 2:
                        exl.wait(eng, g, hg - 2)
                    else:
                        exl.wait(eng, g - 1, 2 + hg)
                    eng.matmul(sbk[:, 0:n], identb[:, :], band[:, 0 if t == 0 else 1, :, :]
                               .rearrange("p h j -> p (h j)"), start=True, stop=False, skip_group_check=True)
                    for pl in range(2):
                        pr = 2 * hg + pl
                        for grp in range(2):
                            k0 = t * P + grp * GRP
                            m = eng.matmul(sbk[grp * GRP:(grp + 1) * GRP, pl * 2 * SPAN:(pl + 1) * 2 * SPAN],
                                           QTL[:, pr, grp * GRP:(grp + 1) * GRP], KZL[:, pr, :, k0:k0 + SPAN],
                                           start=False, stop=(pl == 1), skip_group_check=True)
                    scl.inc(m)

            def local_softmax(name, eng, s, t, hg):
                g = s * TPB + t
                s3 = bank[2 + hg % 2][:, 0:HG * SPAN].rearrange("p (h j) -> p h j", h=HG)
                pl = PL[hg % 2]
                cols = slice(HG * hg, HG * hg + HG)
                if name == "dve":
                    scl.wait(eng, g, hg)
                    exl.wait(eng, g - 1, hg)
                    nml.inc(eng.tensor_reduce(NML[:, cols], s3, AX.X, ALU.max, negate=True))
                if name == "act":
                    nml.wait(eng, g, hg)
                    ril.wait(eng, g - 1, hg)
                    if hg >= 2:
                        ptl.wait(eng, g, hg - 2)
                    else:
                        ptl.wait(eng, g - 1, 2 + hg)
                    for h in range(HG):
                        c = HG * hg + h
                        i = eng.activation(pl[:, h, :], s3[:, h, :], ACT.Exp, bias=NML[:, c:c + 1],
                                           accum_out=RSL[:, c:c + 1])
                    exl.inc(i)

            def local_normalise(name, eng, s, t, hg):
                g = s * TPB + t
                cols = slice(HG * hg, HG * hg + HG)
                if name == "dve":
                    exl.wait(eng, g, hg)
                    pnl.wait(eng, g - 1, hg)
                    ril.inc(eng.reciprocal(RIL[:, cols], RSL[:, cols]))
                if name == "pool":
                    ril.wait(eng, g, hg)
                    pl = PL[hg % 2]
                    r = RIL[:, cols].rearrange("p (h a) -> p h a", a=1).to_broadcast([P, HG, SPAN])
                    pnl.inc(eng.tensor_tensor(pl[:, :, :], pl[:, :, :], r, ALU.mult))

            def local_transpose(name, eng, s, t, hg):
                g = s * TPB + t
                if name == "pe":
                    pnl.wait(eng, g, hg)
                    if hg:
                        pcl.wait(eng, g, hg - 1)
                    else:
                        pcl.wait(eng, g - 1)
                    for h in range(HG):
                        i = eng.transpose(bank[4][0:SPAN, h * P:(h + 1) * P], PL[hg % 2][:, h, :], ident[:, :])
                    ptl.inc(i)
                if name == "dve":
                    ptl.wait(eng, g, hg)
                    if hg >= 2:
                        avl.wait(eng, g, hg - 2)
                    else:
                        avl.wait(eng, g - 1, 2 + hg)
                    pcl.inc(eng.tensor_copy(PTL[hg % 2][:, :], bank[4][0:SPAN, :]))

            def local_av(name, eng, s, t, hg):
                g = s * TPB + t
                if name == "pe":
                    pcl.wait(eng, g, hg)
                    if hg == 0:
                        cv.wait(eng, g)
                        ovl.wait(eng, g - 1)
                        fin.wait(eng, s - 1)
                    if hg == 2:
                        ovl.wait(eng, g, 0)
                    for h in range(HG):
                        head = HG * hg + h
                        pl, e = divmod(head % 8, 2)
                        for grp in range(2):
                            o0 = pl * P + grp * GRP
                            i = eng.matmul(bank[6][e * DH:(e + 1) * DH, o0:o0 + GRP],
                                           VG[t % 2][:, grp, head * DH:(head + 1) * DH],
                                           PTL[hg % 2][:, h * P + grp * GRP:h * P + (grp + 1) * GRP],
                                           start=True, stop=True)
                    avl.inc(i)
                if name == "act" and hg % 2:
                    avl.wait(eng, g, hg)
                    yl.wait(eng, g - 1)
                    ovl.inc(eng.activation(OTL[:, 2 * hg - 2:2 * hg + 2, :],
                                           bank[6][:, :].rearrange("p (i q) -> p i q", i=4), ACT.Copy))

            def local_out(name, eng, s, t, nxt=True):
                g = s * TPB + t
                lp = (s // BATCH) % 2
                if name == "pe":
                    ovl.wait(eng, g)
                    if nxt:
                        fxd.wait(eng, g + 1)
                        fxa.wait(eng, g + 1)
                    else:
                        x2.wait(eng, g - 1)
                    for pr in range(PAIRS):
                        i = eng.matmul(bank[7][:, 0:E], OTL[:, pr, :], WO[:, lp, pr, :],
                                       start=(pr == 0), stop=(pr == PAIRS - 1))
                    yl.inc(i)
                if name == "dve":
                    yl.wait(eng, g)
                    fin.wait(eng, s - 1)
                    g1.wait(eng, s - 1)
                    x2b.wait(eng, g - 1)
                    x2.inc(eng.tensor_tensor(X2[:, t, :], bank[7][:, 0:E], X[:, (s % BATCH) * TPB + t, :], ALU.add))
                if name == "pool":
                    x2.wait(eng, g)
                    settle(eng)
                    x2b.inc(eng.tensor_tensor(X2B[:, t, :], X2[:, t, :], B2[:, lp, :], ALU.add))

            def ffn(name, eng, s):
                lp = (s // BATCH) % 2
                m = bank[7]
                m3 = m[:, :].rearrange("p (t e) -> p t e", t=TPB)
                if name == "pe":
                    x2.wait(eng, s * TPB + TPB - 1)
                    for t in range(TPB):
                        i = eng.transpose(m[:, t * P:(t + 1) * P], X2[:, t, :], ident[:, :])
                    g1.inc(i)
                    g1d.wait(eng, s)
                    g1a.wait(eng, s)
                    for t in range(TPB):
                        i = eng.transpose(m[:, t * P:(t + 1) * P], XT2[:, t * P:(t + 1) * P], ident[:, :])
                    g2.inc(i)
                    gxn.wait(eng, s)
                    for t in range(TPB):
                        i = eng.transpose(m[:, t * P:(t + 1) * P], XN[:, t, :], ident[:, :])
                    g3.inc(i)
                    gxt.wait(eng, s)
                if name == "dve":
                    g1.wait(eng, s)
                    g1d.inc(eng.tensor_copy(XT2[0:DH, 0:SEQ], m[0:DH, :]))
                    g2.wait(eng, s)
                    for t in range(TPB):
                        gst.inc(eng.bn_stats(stats[:, t, :], m3[:, t, :]))
                    gst.wait(eng, s, TPB - 1)
                    settle(eng)
                    for t in range(TPB):
                        i = eng.bn_aggr(mv[:, t, :], stats[:, t, :])
                    gst.inc(i)
                    gst.wait(eng, s)
                    gve.inc(eng.tensor_scalar(veps[:, :], mv[:, :, 1], LN_EPS, None, ALU.add))
                    grs.wait(eng, s)
                    for t in range(TPB):
                        i = eng.tensor_scalar(XN[:, t, :], m3[:, t, :], mv[:, t, 0:1], rstd[:, t:t + 1],
                                              ALU.subtract, ALU.mult)
                    gxn.inc(i)
                if name == "pool":
                    gve.wait(eng, s)
                    grs.inc(eng.tensor_tensor(rstd[:, :], veps[:, :], mhalf[:, 0:TPB], ALU.pow))
                if name == "act":
                    g1.wait(eng, s)
                    g1a.inc(eng.activation(XT2[DH:P, 1:SEQ + 1], m[DH:P, :], ACT.Copy))
                    g3.wait(eng, s)
                    gsel = GBA[:, 0, bass.ds(s // BATCH, 1)]
                    bsel = GBA[:, 1, bass.ds(s // BATCH, 1)]
                    gxt.inc(eng.activation(XNT2[:, :], m[:, :], ACT.Identity, scale=gsel, bias=bsel))

                for t in range(TPB + 1):
                    if t < TPB:
                        ffn_up(name, eng, s, t, lp)
                    if t > 0:
                        ffn_down(name, eng, s, t - 1, lp)

            def ffn_up(name, eng, s, t, lp):
                up = (bank[2], bank[3]) if t % 2 == 0 else (bank[0], bank[1])
                if name == "pe":
                    if t == 0:
                        exl.wait(eng, s * TPB + TPB - 1)
                    if t == 1:
                        cv_last(eng, s)
                    for k in range(2):
                        if t >= 2:
                            hb.wait(eng, s, 2 * (t - 2) + k)
                        i = eng.matmul(up[k][:, 0:FF], XNT2[:, t * P:(t + 1) * P],
                                       W1[:, lp, k * FF:(k + 1) * FF], start=True, stop=True)
                        hh.inc(i)
                if name == "dve":
                    hh.wait(eng, s, 2 * t)
                    if t >= 2:
                        ht.wait(eng, s, t - 2)
                    else:
                        ht.wait(eng, s - 1, 2 + t)
                    hb.inc(eng.tensor_tensor(A1[t % 2][:, :], up[0][:, 0:FF], B1[:, lp, 0:FF], ALU.add))
                    hh.wait(eng, s, 2 * t + 1)
                    if t >= 2:
                        hm.wait(eng, s, t - 2)
                    else:
                        hm.wait(eng, s - 1, 2 + t)
                    hb.inc(eng.tensor_tensor(G1[t % 2][:, :], up[1][:, 0:FF], B1[:, lp, FF:2 * FF], ALU.add))
                if name == "act":
                    hb.wait(eng, s, 2 * t + 1)
                    ge.inc(eng.activation(G1[t % 2][:, :], G1[t % 2][:, :], ACT.Gelu))
                if name == "pool":
                    ge.wait(eng, s, t)
                    hb.wait(eng, s, 2 * t)
                    hm.inc(eng.tensor_tensor(A1[t % 2][:, :], A1[t % 2][:, :], G1[t % 2][:, :], ALU.mult))

            def cv_last(eng, s):
                cv.wait(eng, s * TPB + TPB - 1)
                if not isinstance(s, int) or s < STEPS - 1:
                    cv.wait(eng, (s + 1) * TPB)

            def ffn_down(name, eng, s, t, lp):
                tb = bank[5]
                yb = bank[6 + t % 2]
                if name == "pe":
                    hm.wait(eng, s, t)
                    if t == 0:
                        ke0.wait(eng, s * TPB + TPB - 1)
                        ke1.wait(eng, s * TPB + TPB - 1)
                        ovl.wait(eng, s * TPB + TPB - 1)
                    else:
                        he.wait(eng, s, t - 1)
                    for c, (c0, n) in enumerate(FFC):
                        i = eng.transpose(tb[0:n, c * P:(c + 1) * P], A1[t % 2][:, c0:c0 + n], ident[:, :])
                    ht.inc(i)
                    he.wait(eng, s, t)
                    if t >= 2:
                        fin.wait(eng, s, t - 2)
                    for c, (c0, n) in enumerate(FFC):
                        i = eng.matmul(yb[:, 0:E], HT[0:n, c, :], W2[0:n, lp, c, :],
                                       start=(c == 0), stop=(c == len(FFC) - 1))
                    fy.inc(i)
                if name == "act":
                    ht.wait(eng, s, t)
                    if t:
                        fy.wait(eng, s, t - 1)
                    else:
                        fy.wait(eng, s - 1)
                    nf = len(FFC) - 1
                    n = FFC[nf][1]
                    eng.activation(HT[:, 0:nf, :], tb[:, 0:nf * P].rearrange("p (c q) -> p c q", c=nf), ACT.Copy)
                    he.inc(eng.activation(HT[0:n, nf, :], tb[0:n, nf * P:(nf + 1) * P], ACT.Copy))
                if name == "dve":
                    fy.wait(eng, s, t)
                    x2b.wait(eng, s * TPB + t)
                    fin.inc(eng.tensor_tensor(X[:, (s % BATCH) * TPB + t, :], yb[:, 0:E], X2B[:, t, :], ALU.add))

            def slot(name, eng, s, t, nxt=True):
                fs, ft = (s, t + 1) if t < TPB - 1 else (s + 1, 0)

                def front(c):
                    if nxt:
                        front_chunk(name, eng, fs, ft, c)

                def rotary(c):
                    if nxt:
                        front_rotary(name, eng, fs, ft, c)

                a = (name, eng, s, t)
                if nxt and ft == 0:
                    rotary_tables(name, eng, fs)
                feature_major(*a, 0)
                if nxt:
                    front_x(name, eng, fs, ft)
                feature_major(*a, 1)
                front(0)
                feature_major(*a, 2)
                front(1)
                local_scores(*a, 0)
                local_softmax(*a, 0)
                feature_major(*a, 3)
                rotary(0)
                local_normalise(*a, 0)
                local_scores(*a, 1)
                local_softmax(*a, 1)
                front(2)
                rotary(1)
                local_normalise(*a, 1)
                local_transpose(*a, 0)
                local_scores(*a, 2)
                local_softmax(*a, 2)
                local_av(*a, 0)
                front(3)
                rotary(2)
                local_normalise(*a, 2)
                local_transpose(*a, 1)
                local_scores(*a, 3)
                local_softmax(*a, 3)
                local_av(*a, 1)
                front(4)
                rotary(3)
                front(5)
                local_normalise(*a, 3)
                local_transpose(*a, 2)
                front(6)
                local_av(*a, 2)
                local_transpose(*a, 3)
                front(7)
                local_av(*a, 3)
                local_out(*a, nxt)

            def step(name, eng, s, last=False):
                for t in range(TPB):
                    slot(name, eng, s, t, nxt=not (last and t == TPB - 1))
                ffn(name, eng, s)

            def layers_program(name, eng):
                if name == "sp":
                    in_dma(eng, s_i, ROT[:, :, :, :], rot.rearrange("k (t p) d -> p k t d", p=P))
                    in_dma(eng, s_i, LGB[0:DEPTH, :], lng)
                    in_dma(eng, s_i, LGB[DEPTH:2 * DEPTH, :], lnb)
                    for l in range(DEPTH):
                        if l >= 2:
                            fin.wait(eng, (l - 1) * BATCH - 1)
                            rtd.wait(eng, (l - 1) * BATCH)
                        load_layer(eng, l, l % 2, s_w)
                        eng.wait_ge(s_w, (l + 1) * 16 * NW)
                    eng.wait_ge(s_i, 48)
                    return
                if name == "pool":
                    eng.memset(KZL[:, :, :, :], 0.0).then_inc(s_k, 1)
                    eng.memset(XT[:, :], 0.0).then_inc(s_k, 1)
                    eng.memset(XT2[:, :], 0.0).then_inc(s_k, 1)
                    eng.memset(band[:, :, :, :], 0.0).then_inc(s_k, 1)
                    eng.wait_ge(s_k, 4)
                    n = 0
                    for grp in range(2):
                        rows = slice(grp * GRP, (grp + 1) * GRP)
                        bm = band[rows, :, :, :].rearrange("p k h j -> p (k h) j")
                        eng.affine_select(out=bm, in_=bm, compare_op=ALU.is_ge, fill=FORBID, base=0,
                                          pattern=[[0, 2 * HG], [1, SPAN]], channel_multiplier=-1).then_inc(s_k, 1)
                        n += 1
                        eng.wait_ge(s_k, 4 + n)
                        eng.affine_select(out=bm, in_=bm, compare_op=ALU.is_ge, fill=FORBID, base=WIN,
                                          pattern=[[0, 2 * HG], [-1, SPAN]], channel_multiplier=1).then_inc(s_k, 1)
                        n += 1
                        eng.wait_ge(s_k, 4 + n)
                    eng.memset(band[0:GRP, 0, :, 0:WIN], FORBID).then_inc(s_k, 1)
                if name == "dve":
                    i = eng.tensor_copy(XM[:, :, :], X[:, :, :])
                    i.then_inc(s_m, 1)
                    eng.wait_ge(s_m, 1)
                with_ln = ln2
                if name in ("dve", "pool"):
                    with eng.Fori(0, BATCH) as b:
                        with_ln(name, eng, b)
                if name == "pool":
                    lx.wait(eng, BATCH - 1)
                if name != "sp":
                    eng.wait_ge(s_k, 9)
                    eng.wait_ge(s_i, 48)
                ln_gains(name, eng)
                rotary_tables(name, eng, 0)
                front_x(name, eng, 0, 0)
                for c in range(8):
                    front_chunk(name, eng, 0, 0, c)
                for c in range(4):
                    front_rotary(name, eng, 0, 0, c)
                with eng.Fori(0, STEPS - 1) as s:
                    step(name, eng, s)
                step(name, eng, STEPS - 1, last=True)

            lst = sig("lst", 5, "dve")
            lve = sig("lve", 1, "dve")
            lrs = sig("lrs", 1, "pool")
            lx = sig("lx", 4, "dve")

            def ln2(name, eng, b):
                if name == "dve":
                    for t in range(TPB):
                        lst.inc(eng.bn_stats(stats[:, t, :], X[:, b * TPB + t, :]))
                    lst.wait(eng, b, TPB - 1)
                    settle(eng)
                    for t in range(TPB):
                        i = eng.bn_aggr(mv[:, t, :], stats[:, t, :])
                    lst.inc(i)
                    lst.wait(eng, b)
                    lrs.wait(eng, b - 1)
                    lve.inc(eng.tensor_scalar(veps[:, :], mv[:, :, 1], LN_EPS, None, ALU.add))
                    lrs.wait(eng, b)
                    for t in range(TPB):
                        xt = X[:, b * TPB + t, :]
                        lx.inc(eng.tensor_scalar(xt, xt, mv[:, t, 0:1], rstd[:, t:t + 1],
                                                 ALU.subtract, ALU.mult))
                if name == "pool":
                    lve.wait(eng, b)
                    lx.wait(eng, b - 1)
                    lrs.inc(eng.tensor_tensor(rstd[:, :], veps[:, :], mhalf[:, 0:TPB], ALU.pow))

            engines_run(nc, sigs, layers_program)

        with ExitStack() as ctx:
            s_o = ctx.enter_context(nc.semaphore("s_o"))
            s_d = ctx.enter_context(nc.semaphore("s_d"))

            def out_program(name, eng):
                for b in range(BATCH):
                    r = slice(b * TPB, (b + 1) * TPB)
                    if name == "dve":
                        eng.tensor_tensor(XM[:, r, :], XM[:, r, :], X[:, r, :], ALU.add).then_inc(s_o, 1)
                    if name == "sp":
                        eng.wait_ge(s_o, b + 1)
                        eng.dma_start(out_t[:, r, :], XM[:, r, :]).then_inc(s_d, 16)
                if name == "sp":
                    eng.wait_ge(s_d, 16 * BATCH)

            engines_run(nc, (), out_program)


_INS = ['L0_attn_x', 'L0_attn_Wq', 'L0_attn_Wk', 'L0_attn_Wv', 'L0_attn_Wr', 'L0_ffn_Wqkv', 'L0_ffn_q_scale',
        'L0_ffn_k_scale', 'L0_ffn_Wo', 'L0_ffn_ln_g', 'L0_ffn_ln_b', 'L0_ffn_W1', 'L0_ffn_b1', 'L0_ffn_W2',
        'L0_ffn_b2']


def rotary_constants():
    import numpy as np
    f = np.float32
    half = np.arange(0, DH, 2, dtype=f)
    inv_freq = (f(1.0) / np.power(f(10000.0), half / f(DH))).astype(f)
    pos = np.arange(SEQ, dtype=f)
    freqs = (pos[:, None] * inv_freq[None, :]).astype(f)
    freqs = np.concatenate([freqs, freqs], -1).astype(np.float64)
    base = ((half + f(0.4 * DH)) / f(1.4 * DH)).astype(f)
    power = ((pos - SEQ // 2) / f(WIN // 2)).astype(f)
    scale = np.power(base[None, :].astype(np.float64), power[:, None])
    scale = np.concatenate([scale, scale], -1)
    sign = np.where(np.arange(DH) < DH // 2, -1.0, 1.0)
    cos, sin = np.cos(freqs), np.sin(freqs) * sign
    return np.stack([cos * scale * QK_SCALE, sin * scale * QK_SCALE, cos / scale, sin / scale]).astype(f)


def kernel(**inputs):
    import numpy as _np
    import concourse.bacc as _bacc
    from concourse import mybir as _mybir
    from concourse.bass_utils import run_bass_kernel_spmd as _run

    nc = _bacc.Bacc("TRN2", target_bir_lowering=False, num_devices=1)
    arrays, args = {}, []
    for name in _INS:
        arrays[f"in_{name}_dram"] = _np.ascontiguousarray(inputs[name])
    arrays["rotary_dram"] = rotary_constants()
    for name, a in arrays.items():
        args.append(nc.dram_tensor(name, a.shape, _mybir.dt.from_np(a.dtype), kind="ExternalInput").ap())
    args.append(nc.dram_tensor("out_0_dram", (BATCH, SEQ, E), F32, kind="ExternalOutput").ap())
    build(nc, *args)
    r = _run(nc, [arrays], core_ids=[0])
    return r.results[0]["out_0_dram"]
```

```python
from contextlib import ExitStack

import concourse.bass as bass
from concourse import mybir

F32 = mybir.dt.float32
BF16 = mybir.dt.bfloat16
ALU = mybir.AluOpType
ACT = mybir.ActivationFunctionType
AX = mybir.AxisListType

P = 128
E = 128
HEADS = 16
DH = 64
INNER = HEADS * DH
PAIRS = HEADS // 2
BATCH = 4
SEQ = 512
TPB = SEQ // P
TILES = BATCH * TPB
DEPTH = 6
WIN = 32
GRP = 2 * WIN
SPAN = GRP + WIN
HG = 4
NHG = HEADS // HG
FF = int(E * 4 * 2 / 3)
FFC = [(c, min(P, FF - c)) for c in range(0, FF, P)]
STEPS = DEPTH * BATCH
PENALTY = -50.0
FORBID = -1e25
SCALE = 0.125
QK_SCALE = 8.0
LN_EPS = 1e-5
NORM2_EPS = 1e-24


class Sig:

    def __init__(self, nc, ctx, name, per, owner, lag=1):
        self.sem = ctx.enter_context(nc.semaphore(name))
        self.per, self.owner, self.lag = per, owner, lag

    def start(self, engine):
        engine.sem_inc(self.sem, self.lag * self.per)

    def inc(self, ins):
        ins.then_inc(self.sem, 1)

    def wait(self, engine, unit, event=None):
        n = self.per - 1 if event is None else event
        engine.wait_ge(self.sem, (unit + self.lag) * self.per + n + 1)


def engines_run(nc, sigs, program):
    with nc.Block() as block:
        for name, deco in (("pe", block.tensor), ("act", block.scalar), ("dve", block.vector),
                           ("pool", block.gpsimd), ("sp", block.sync)):
            def body(eng, name=name):
                for s in sigs:
                    if s.owner == name:
                        s.start(eng)
                program(name, eng)
            deco(body)


def build(nc, x, wq, wk, wv, wr, wqkv, qscale, kscale, wo, lng, lnb, w1, b1, w2, b2, rot, out):
    with ExitStack() as keep:
        def sb(name, shape, dt=F32, ctx=keep):
            return ctx.enter_context(nc.sbuf_tensor(name, shape, dt))

        bank = [keep.enter_context(nc.psum_tensor(f"bank{i}", [P, 512], F32)) for i in range(8)]
        X = sb("X", [P, TILES, E])
        XM = sb("XM", [P, TILES, E])
        ident = sb("ident", [P, P])
        s_c = keep.enter_context(nc.semaphore("s_const"))

        passed = {}

        def settle(eng):
            k = str(eng.engine)
            if k not in passed:
                passed[k] = keep.enter_context(nc.semaphore(f"passed{len(passed)}"))
            eng.sem_inc(passed[k], 1)

        identb = sb("identb", [P, P], BF16)
        stats = sb("stats", [P, TPB, 6])
        mv = sb("mv", [P, TPB, 2])
        veps = sb("veps", [P, TPB])
        rstd = sb("rstd", [P, TPB])
        mhalf = sb("mhalf", [P, 64])

        def in_dma(engine, sem, dst, src):
            engine.dma_start(dst, src).then_inc(sem, 16)

        x_t = x.rearrange("b (t p) e -> p (b t) e", p=P)
        out_t = out.rearrange("b (t p) e -> p (b t) e", p=P)

        with ExitStack() as ctx:
            def sbl(name, shape, dt=F32):
                return sb(name, shape, dt, ctx)

            W0 = sbl("W0", [P, 3, INNER])
            WR = sbl("WR", [P, PAIRS, E])
            XNT = sbl("XNT", [P, BATCH * SEQ])
            XN0 = sbl("XN0", [P, TPB, E])
            WP = [sbl(f"WP{i}", [P, 3, P]) for i in range(2)]
            XNS = [sbl(f"XNS{i}", [P, SEQ]) for i in range(2)]
            QT = [sbl(f"QT{i}", [P, SEQ]) for i in range(2)]
            KZ = [sbl(f"KZ{i}", [P, 2, SEQ]) for i in range(2)]
            V = [sbl(f"V{i}", [P, TPB, P]) for i in range(2)]
            PR = [sbl(f"PR{i}", [P, SEQ]) for i in range(2)]
            PTS = [[sbl(f"PTS{i}{e}", [P, TPB, SEQ]) for e in range(2)] for i in range(2)]
            OT = sbl("OT", [P, SEQ])
            NM = sbl("NM", [P, 8])
            RS = sbl("RS", [P, 8])
            RI = sbl("RI", [P, 8])
            causal = sbl("causal", [P, SEQ], BF16)

            s_in = ctx.enter_context(nc.semaphore("s_x"))
            s_w0 = ctx.enter_context(nc.semaphore("s_w0"))
            lnst = Sig(nc, ctx, "lnst", 5, "dve")
            lnve = Sig(nc, ctx, "lnve", 1, "dve")
            lnrs = Sig(nc, ctx, "lnrs", 1, "pool")
            lnxn = Sig(nc, ctx, "lnxn", 4, "dve")
            lntr = Sig(nc, ctx, "lntr", 1, "pe")
            lnev = Sig(nc, ctx, "lnev", 1, "act")

            def ln_program(name, eng):
                if name == "sp":
                    for i in range(2):
                        in_dma(eng, s_in, X[:, 8 * i:8 * i + 8, :], x_t[:, 8 * i:8 * i + 8, :])
                    for i, w in enumerate((wq, wk, wv)):
                        in_dma(eng, s_w0, W0[:, i, :], w)
                    in_dma(eng, s_w0, WR[:, :, :], wr.rearrange("(c p) e -> p c e", p=P))
                    eng.wait_ge(s_w0, 64)
                if name == "pool":
                    eng.memset(ident[:, :], 0.0).then_inc(s_c, 1)
                    eng.memset(identb[:, :], 0.0).then_inc(s_c, 1)
                    eng.memset(causal[:, :], 0.0).then_inc(s_c, 1)
                    eng.memset(mhalf[:, :], -0.5).then_inc(s_c, 1)
                    for i in range(2):
                        eng.memset(KZ[i][:, :, :], 0.0).then_inc(s_c, 1)
                    eng.wait_ge(s_c, 6)
                    for m in (ident, identb):
                        eng.affine_select(out=m[:, :], in_=m[:, :], compare_op=ALU.not_equal, fill=1.0,
                                          base=0, pattern=[[-1, P]], channel_multiplier=1).then_inc(s_c, 1)
                    eng.affine_select(out=causal[:, :], in_=causal[:, :], compare_op=ALU.is_ge,
                                      fill=PENALTY, base=0, pattern=[[-1, SEQ]],
                                      channel_multiplier=1).then_inc(s_c, 1)
                if name == "sp":
                    return
                with eng.Fori(0, BATCH) as b:
                    if name == "dve":
                        eng.wait_ge(s_in, 32)
                        for t in range(TPB):
                            lnst.inc(eng.bn_stats(stats[:, t, :], X[:, b * TPB + t, :]))
                        for t in range(TPB):
                            lnst.wait(eng, b, t)
                            settle(eng)
                            i = eng.bn_aggr(mv[:, t, :], stats[:, t, :])
                        lnst.inc(i)
                        lnst.wait(eng, b)
                        lnrs.wait(eng, b - 1)
                        lnve.inc(eng.tensor_scalar(veps[:, :], mv[:, :, 1], LN_EPS, None, ALU.add))
                        lnrs.wait(eng, b)
                        lntr.wait(eng, b - 1)
                        for t in range(TPB):
                            lnxn.inc(eng.tensor_scalar(XN0[:, t, :], X[:, b * TPB + t, :], mv[:, t, 0:1],
                                                       rstd[:, t:t + 1], ALU.subtract, ALU.mult))
                    if name == "pool":
                        eng.wait_ge(s_c, 9)
                        lnve.wait(eng, b)
                        lnrs.inc(eng.tensor_tensor(rstd[:, :], veps[:, :], mhalf[:, 0:TPB], ALU.pow))
                    if name == "pe":
                        eng.wait_ge(s_c, 9)
                        lnxn.wait(eng, b)
                        lnev.wait(eng, b - 1)
                        for t in range(TPB):
                            i = eng.transpose(bank[7][:, t * P:(t + 1) * P], XN0[:, t, :], ident[:, :])
                        lntr.inc(i)
                    if name == "act":
                        lntr.wait(eng, b)
                        lnev.inc(eng.activation(XNT[:, bass.ds(b * SEQ, SEQ)], bank[7][:, :], ACT.Copy))

            engines_run(nc, (lnst, lnve, lnrs, lnxn, lntr, lnev), ln_program)

            NJ = 2 * TPB
            wps = Sig(nc, ctx, "wps", 2, "pool")
            pj = Sig(nc, ctx, "pj", 3, "pe")
            pja = Sig(nc, ctx, "pja", 3, "act")
            pjd = Sig(nc, ctx, "pjd", 1, "dve")
            sc = Sig(nc, ctx, "sc", NJ, "pe", 2)
            nm = Sig(nc, ctx, "nm", NJ, "dve")
            ex = Sig(nc, ctx, "ex", NJ, "act")
            ri = Sig(nc, ctx, "ri", NJ, "dve")
            pn = Sig(nc, ctx, "pn", NJ, "dve")
            pt = Sig(nc, ctx, "pt", NJ, "pe")
            pe = Sig(nc, ctx, "ptc", NJ, "dve")
            av = Sig(nc, ctx, "av", 1, "pe", 2)
            ov = Sig(nc, ctx, "ov", 1, "act")
            yy = Sig(nc, ctx, "yy", 1, "pe")
            xa = Sig(nc, ctx, "xa", 1, "dve")
            sigs0 = (wps, pj, pja, pjd, sc, nm, ex, ri, pn, pt, pe, av, ov, yy, xa)

            def stage(name, eng, u, par):
                if name == "pool":
                    pj.wait(eng, u - 1)
                    w = eng.tensor_copy(WP[par][:, :, :], W0[:, :, bass.ds((u % PAIRS) * P, P)])
                    wps.inc(w)
                    wps.inc(eng.tensor_copy(XNS[par][:, :], XNT[:, bass.ds((u // PAIRS) * SEQ, SEQ)]))

            def project(name, eng, u, par, c):
                pb = bank[c % 2]
                if name == "pe":
                    wps.wait(eng, u)
                    if c == 0:
                        pja.wait(eng, u - 1, 2)
                        eng.matmul(pb[:, :], WP[par][:, 0, :], XNS[par][:, :], start=True, stop=True)\
                           .then_inc(pj.sem, 1)
                    if c == 1:
                        pja.wait(eng, u - 1, 1)
                        pjd.wait(eng, u - 1)
                        eng.matmul(pb[:, :], WP[par][:, 1, :], XNS[par][:, :], start=True, stop=True)\
                           .then_inc(pj.sem, 1)
                    if c == 2:
                        pja.wait(eng, u, 0)
                        for t in range(TPB):
                            i = eng.matmul(pb[:, t * P:(t + 1) * P], XNS[par][:, t * P:(t + 1) * P],
                                           WP[par][:, 2, :], start=True, stop=True)
                        pj.inc(i)
                if name == "act":
                    pj.wait(eng, u, c)
                    if c == 0:
                        sc.wait(eng, u - 2)
                        pja.inc(eng.activation(QT[par][:, :], pb[:, :], ACT.Copy))
                    if c == 1:
                        pja.inc(eng.activation(KZ[par][DH:P, 1, :], pb[DH:P, :], ACT.Copy, scale=SCALE))
                    if c == 2:
                        av.wait(eng, u - 2)
                        pja.inc(eng.activation(V[par][:, :, :], pb[:, :].rearrange("p (t d) -> p t d", t=TPB),
                                               ACT.Copy))
                if name == "dve" and c == 1:
                    pj.wait(eng, u, 1)
                    sc.wait(eng, u - 2)
                    pjd.inc(eng.tensor_scalar(KZ[par][0:DH, 0, :], pb[0:DH, :], SCALE, None, ALU.mult))

            def scores(name, eng, u, par, j):
                qt, e = divmod(j, 2)
                sbk = bank[2 + j % 2]
                if name == "pe":
                    pja.wait(eng, u, 1)
                    pjd.wait(eng, u)
                    if j >= 2:
                        ex.wait(eng, u, j - 2)
                    else:
                        ex.wait(eng, u - 1, NJ - 2 + j)
                    eng.matmul(sbk[:, :], QT[par][:, qt * P:(qt + 1) * P], KZ[par][:, e, :],
                               start=True, stop=False, skip_group_check=True)
                    sc.inc(eng.matmul(sbk[:, qt * P:SEQ], identb[:, :], causal[:, 0:SEQ - qt * P],
                                      start=False, stop=True, skip_group_check=True))

            def softmax(name, eng, u, par, j):
                sbk = bank[2 + j % 2]
                if name == "dve":
                    sc.wait(eng, u, j)
                    ex.wait(eng, u - 1, j)
                    nm.inc(eng.tensor_reduce(NM[:, j:j + 1], sbk[:, :], AX.X, ALU.max, negate=True))
                if name == "act":
                    nm.wait(eng, u, j)
                    ri.wait(eng, u - 1, j)
                    if j >= 2:
                        pt.wait(eng, u, j - 2)
                    else:
                        pt.wait(eng, u - 1, NJ - 2 + j)
                    ex.inc(eng.activation(PR[j % 2][:, :], sbk[:, :], ACT.Exp, bias=NM[:, j:j + 1],
                                          accum_out=RS[:, j:j + 1]))

            def normalise(name, eng, u, par, j):
                if name == "dve":
                    ex.wait(eng, u, j)
                    pn.wait(eng, u - 1, j)
                    ri.inc(eng.reciprocal(RI[:, j:j + 1], RS[:, j:j + 1]))
                    ri.wait(eng, u, j)
                    pn.inc(eng.tensor_scalar(PR[j % 2][:, :], PR[j % 2][:, :], RI[:, j:j + 1], None, ALU.mult))

            def transpose_p(name, eng, u, par, j):
                qt, e = divmod(j, 2)
                tb = bank[4 + j % 2]
                if name == "pe":
                    pn.wait(eng, u, j)
                    if j >= 2:
                        pe.wait(eng, u, j - 2)
                    else:
                        pe.wait(eng, u - 1, NJ - 2 + j)
                    for k in range(TPB):
                        i = eng.transpose(tb[:, k * P:(k + 1) * P], PR[j % 2][:, k * P:(k + 1) * P], ident[:, :])
                    pt.inc(i)
                if name == "dve":
                    pt.wait(eng, u, j)
                    av.wait(eng, u - 2)
                    pe.inc(eng.tensor_copy(PTS[par][e][:, :, qt * P:(qt + 1) * P],
                                           tb[:, :].rearrange("p (k q) -> p k q", k=TPB)))

            def times_v(name, eng, u, par):
                if name == "pe":
                    pja.wait(eng, u, 2)
                    pe.wait(eng, u)
                    ov.wait(eng, u - 1)
                    for k in range(TPB):
                        for e in range(2):
                            i = eng.matmul(bank[6][e * DH:(e + 1) * DH, :], V[par][:, k, e * DH:(e + 1) * DH],
                                           PTS[par][e][:, k, :], start=(k == 0), stop=(k == TPB - 1))
                    av.inc(i)
                if name == "act":
                    av.wait(eng, u)
                    yy.wait(eng, u - 1)
                    ov.inc(eng.activation(OT[:, :], bank[6][:, :], ACT.Copy))

            def project_out(name, eng, u, par):
                if name == "pe":
                    ov.wait(eng, u)
                    xa.wait(eng, u - 1)
                    for t in range(TPB):
                        i = eng.matmul(bank[7][:, t * P:(t + 1) * P], OT[:, t * P:(t + 1) * P],
                                       WR[:, u % PAIRS, :], start=True, stop=True)
                    yy.inc(i)
                if name == "dve":
                    yy.wait(eng, u)
                    xa.wait(eng, u - 1)
                    xs = X[:, bass.ds((u // PAIRS) * TPB, TPB), :]
                    xa.inc(eng.tensor_tensor(xs, xs, bank[7][:, :].rearrange("p (t e) -> p t e", t=TPB), ALU.add))

            def pair(name, eng, u, par, nxt=True):
                for j in range(NJ):
                    if j == 0 and nxt:
                        stage(name, eng, u + 1, 1 - par)
                    if j + 2 < NJ:
                        scores(name, eng, u, par, j + 2)
                    elif nxt and j + 2 == NJ:
                        scores(name, eng, u + 1, 1 - par, 0)
                    if j + 2 < NJ:
                        softmax(name, eng, u, par, j + 2)
                    elif nxt and j + 2 == NJ:
                        softmax(name, eng, u + 1, 1 - par, 0)
                    transpose_p(name, eng, u, par, j)
                    if j + 2 < NJ:
                        normalise(name, eng, u, par, j + 2)
                    elif nxt and j + 2 == NJ:
                        normalise(name, eng, u + 1, 1 - par, 0)
                    if nxt and j in (1, 2, 3):
                        project(name, eng, u + 1, 1 - par, j - 1)
                times_v(name, eng, u, par)
                if nxt:
                    scores(name, eng, u + 1, 1 - par, 1)
                    softmax(name, eng, u + 1, 1 - par, 1)
                    normalise(name, eng, u + 1, 1 - par, 1)
                project_out(name, eng, u, par)

            def attn_program(name, eng):
                if name == "sp":
                    return
                stage(name, eng, 0, 0)
                for c in range(3):
                    project(name, eng, 0, 0, c)
                for j in range(2):
                    scores(name, eng, 0, 0, j)
                    softmax(name, eng, 0, 0, j)
                    normalise(name, eng, 0, 0, j)
                last = BATCH * PAIRS // 2 - 1
                with eng.Fori(0, last) as v:
                    for par in range(2):
                        pair(name, eng, 2 * v + par, par)
                pair(name, eng, 2 * last, 0)
                pair(name, eng, 2 * last + 1, 1, nxt=False)

            engines_run(nc, sigs0, attn_program)

        with ExitStack() as ctx:
            def sbl(name, shape, dt=F32):
                return sb(name, shape, dt, ctx)

            WQKV = sbl("WQKV", [P, 2, 3 * INNER])
            WO = sbl("WO", [P, 2, PAIRS, E])
            W1 = sbl("W1", [P, 2, 2 * FF])
            W2 = sbl("W2", [P, 2, len(FFC), E])
            QKS = sbl("QKS", [P, 2, 2, DH])
            B1 = sbl("B1", [P, 2, 2 * FF])
            B2 = sbl("B2", [P, 2, E])
            ROT = sbl("ROT", [P, 4, TPB, DH])
            RT = sbl("RT", [P, 4, TPB, DH])
            band = sbl("band", [P, 2, HG, SPAN], BF16)

            XS = [sbl(f"XS{i}", [P, E]) for i in range(2)]
            XT = sbl("XT", [P, SEQ + 1])
            QR = sbl("QR", [P, 4, 512])
            SQ = [sbl(f"SQ{i}", [P, 512]) for i in range(2)]
            T2 = [sbl(f"T2{i}", [P, 512]) for i in range(2)]
            TQ = sbl("TQ", [P, 4, 512])
            SS = sbl("SS", [P, 4, 8])
            SM = sbl("SM", [P, 4, 8])
            RN = sbl("RN", [P, 4, 8])
            VN = [sbl(f"VN{i}", [P, INNER]) for i in range(2)]
            VG = [sbl(f"VG{i}", [SPAN, 2, INNER]) for i in range(2)]
            none = sbl("none", [WIN, INNER])
            QTL = sbl("QTL", [P, PAIRS, P])
            KZL = sbl("KZL", [P, PAIRS, 2, WIN + SEQ])
            PL = [sbl(f"PL{i}", [P, HG, SPAN]) for i in range(2)]
            NML = sbl("NML", [P, HEADS])
            RSL = sbl("RSL", [P, HEADS])
            RIL = sbl("RIL", [P, HEADS])
            PTL = [sbl(f"PTL{i}", [SPAN, HG * P]) for i in range(2)]
            OTL = sbl("OTL", [P, PAIRS, P])
            X2 = sbl("X2", [P, TPB, E])
            X2B = sbl("X2B", [P, 2, TPB, E])
            XT2 = sbl("XT2", [P, SEQ + 1])
            XN = sbl("XN", [P, TPB, E])
            XNT2 = sbl("XNT2", [P, SEQ])
            A1 = sbl("A1", [P, TPB, FF])
            G1 = sbl("G1", [P, TPB, FF])
            HT = [sbl(f"HT{i}", [P, len(FFC), P]) for i in range(2)]

            s_i = ctx.enter_context(nc.semaphore("s_i"))
            s_k = ctx.enter_context(nc.semaphore("s_k"))
            s_m = ctx.enter_context(nc.semaphore("s_m"))
            s_w = ctx.enter_context(nc.semaphore("s_w"))
            NW = 10

            def sig(name, per, owner, lag=1):
                s = Sig(nc, ctx, "l_" + name, per, owner, lag)
                sigs.append(s)
                return s
            sigs = []
            xs = sig("xs", 1, "pool")
            fx = sig("fx", 1, "pe")
            fxd = sig("fxd", 1, "dve")
            fxa = sig("fxa", 1, "act")
            ch = sig("ch", 6, "pe")
            cv = sig("cv", 6, "act")
            sq = sig("sq", 4, "act")
            ss = sig("ss", 4, "dve")
            sm = sig("sm", 2, "dve")
            rn = sig("rn", 2, "pool")
            t1 = sig("t1", 4, "dve")
            t2 = sig("t2", 4, "pool")
            ad = sig("ad", 4, "dve")
            qn = sig("qn", 4, "dve")
            tr = sig("tr", 4, "pe")
            qe = sig("qe", 2, "act")
            ke0 = sig("ke0", 2, "dve")
            ke1 = sig("ke1", 2, "act")
            scl = sig("scl", NHG, "pe")
            nml = sig("nml", NHG, "dve")
            exl = sig("exl", NHG, "act")
            ril = sig("ril", NHG, "dve")
            pnl = sig("pnl", NHG, "dve")
            ptl = sig("ptl", NHG, "pe")
            pcl = sig("pcl", NHG, "act")
            avl = sig("avl", NHG, "pe", 2)
            ovl = sig("ovl", 2, "act")
            yl = sig("yl", 1, "pe")
            x2 = sig("x2", 1, "dve", 2)
            x2b = sig("x2b", 1, "pool", TPB)
            rtd = sig("rtd", 2, "dve")
            rtp = sig("rtp", 4, "pool")
            g1 = sig("g1", 1, "pe")
            g1d = sig("g1d", 1, "dve")
            g1a = sig("g1a", 1, "act")
            g2 = sig("g2", 1, "pe")
            gst = sig("gst", 5, "dve")
            gve = sig("gve", 1, "dve")
            grs = sig("grs", 1, "pool")
            gxn = sig("gxn", 1, "dve")
            g3 = sig("g3", 1, "pe")
            gxt = sig("gxt", 1, "act")
            hh = sig("hh", 2 * TPB, "pe")
            hb = sig("hb", 2 * TPB, "dve")
            ge = sig("ge", 1, "act")
            hm = sig("hm", TPB, "pool")
            ht = sig("ht", TPB, "pe")
            he = sig("he", TPB, "act")
            fy = sig("fy", TPB, "pe")
            fin = sig("fin", TPB, "dve", 3)

            def load_layer(eng, l, par, sem):
                at = l if isinstance(l, slice) or not isinstance(l, int) else slice(l, l + 1)

                def one(w):
                    return w[at].rearrange("l r c -> (l r) c")

                def d(dst, src):
                    eng.dma_start(dst, src).then_inc(sem, 16)
                half = 3 * INNER // 2
                for i in range(2):
                    d(WQKV[:, par, i * half:(i + 1) * half], one(wqkv)[:, i * half:(i + 1) * half])
                d(WO[:, par, :, :], one(wo).rearrange("(c p) e -> p c e", p=P))
                d(W1[:, par, :], one(w1))
                c0, n = FFC[-1]
                d(W2[:, par, 0:2, :], one(w2)[0:c0, :].rearrange("(c p) e -> p c e", p=P))
                d(W2[0:n, par, len(FFC) - 1, :], one(w2)[c0:c0 + n, :])
                d(QKS[:, par, 0, :], qscale[at, :].to_broadcast([P, DH]))
                d(QKS[:, par, 1, :], kscale[at, :].to_broadcast([P, DH]))
                d(B1[:, par, :], b1[at, :].to_broadcast([P, 2 * FF]))
                d(B2[:, par, :], b2[at, :].to_broadcast([P, E]))

            def ln_gains(name, eng):
                n = 2 * DEPTH
                if name == "pe":
                    eng.wait_ge(s_i, 48)
                    eng.transpose(bank[5][:, 0:n], LGB[:, :], ident[0:n, 0:n]).then_inc(s_g, 1)
                if name == "dve":
                    eng.wait_ge(s_g, 1)
                    eng.tensor_copy(GBA[:, :, :], bank[5][:, 0:n].rearrange("p (k l) -> p k l", k=2))\
                       .then_inc(s_g, 1)
                if name in ("pe", "act"):
                    eng.wait_ge(s_g, 2)

            LGB = sbl("LGB", [2 * DEPTH, E])
            GBA = sbl("GBA", [P, 2, DEPTH])
            s_g = ctx.enter_context(nc.semaphore("s_g"))

            def rotary_tables(name, eng, s, first=False):
                lp = (s // BATCH) % 2
                if name == "dve":
                    if first:
                        eng.wait_ge(s_i, 48)
                    wait_weights(eng, s)
                    t1.wait(eng, s * TPB - 1)
                    for k in range(2):
                        q = QKS[:, lp, k:k + 1, :].to_broadcast([P, TPB, DH])
                        rtd.inc(eng.tensor_tensor(RT[:, 2 * k, :, :], ROT[:, 2 * k, :, :], q, ALU.mult))
                if name == "pool":
                    if first:
                        eng.wait_ge(s_i, 48)
                    wait_weights(eng, s)
                    t2.wait(eng, s * TPB - 1)
                    settle(eng)
                    for k in range(2):
                        for h in range(2):
                            q = QKS[:, lp, k:k + 1, (1 - h) * 32:(2 - h) * 32].to_broadcast([P, TPB, 32])
                            a = slice(h * 32, h * 32 + 32)
                            rtp.inc(eng.tensor_tensor(RT[:, 2 * k + 1, :, a], ROT[:, 2 * k + 1, :, a], q, ALU.mult))

            def wait_weights(eng, s):
                eng.wait_ge(s_w, (s // BATCH + 1) * 16 * NW)

            def front_x(name, eng, s, t):
                g = s * TPB + t
                b = s % BATCH
                if name == "pool":
                    fx.wait(eng, g - 1)
                    fin.wait(eng, s - 3)
                    xs.inc(eng.tensor_copy(XS[t % 2][:, :], X[:, b * TPB + t, :]))
                if name == "pe":
                    xs.wait(eng, g)
                    x2.wait(eng, g - 2)
                    fx.inc(eng.transpose(bank[7][:, 0:P], XS[t % 2][:, :], ident[:, :]))
                c0 = t * P
                if name == "dve":
                    fx.wait(eng, g)
                    fxd.inc(eng.tensor_copy(XT[0:DH, c0:c0 + P], bank[7][0:DH, 0:P]))
                if name == "act":
                    fx.wait(eng, g)
                    fxa.inc(eng.activation(XT[DH:P, c0 + 1:c0 + 1 + P], bank[7][DH:P, 0:P], ACT.Copy))

            s_v = [ctx.enter_context(nc.semaphore(f"s_v{i}")) for i in range(2)]

            def v_placed(eng, s, t):
                eng.wait_ge(s_v[t % 2], (2 * s + t // 2 + 2) * 48)

            def place_v(name, eng, s, t):
                g = s * TPB + t
                if name == "sp":
                    cv.wait(eng, g)
                    avl.wait(eng, g - 2)
                    v, o = VN[t % 2], VG[t % 2]
                    before = VN[1 - t % 2][P - WIN:P, :] if t else none[:, :]
                    for dst, src in ((o[0:WIN, 0, :], before), (o[WIN:SPAN, 0, :], v[0:GRP, :]),
                                     (o[:, 1, :], v[WIN:P, :])):
                        eng.dma_start(dst, src).then_inc(s_v[t % 2], 16)

            def front_chunk(name, eng, s, t, c):
                g = s * TPB + t
                lp = (s // BATCH) % 2
                pb = bank[c % 2]
                if name == "pe":
                    if c == 0:
                        fxd.wait(eng, g)
                        fxa.wait(eng, g)
                        wait_weights(eng, s)
                    if c >= 2:
                        cv.wait(eng, g, c - 2)
                    else:
                        cv.wait(eng, g - 1, 4 + c)
                    ch.inc(eng.matmul(pb[:, :], XT[:, t * P:(t + 1) * P], WQKV[:, lp, c * 512:(c + 1) * 512],
                                      start=True, stop=True))
                if name == "act":
                    ch.wait(eng, g, c)
                    if c < 4:
                        t1.wait(eng, g - 1, c)
                        t2.wait(eng, g - 1, c)
                        cv.inc(eng.activation(QR[:, c, :], pb[:, :], ACT.Copy))
                    else:
                        if t:
                            v_placed(eng, s, t - 1)
                        else:
                            v_placed(eng, s - 1, TPB - 1)
                        cv.inc(eng.activation(VN[t % 2][:, (c - 4) * 512:(c - 3) * 512], pb[:, :], ACT.Copy))

            def front_products(name, eng, s, t, c):
                g = s * TPB + t
                k = c // 2
                q3 = QR[:, c, :].rearrange("p (h d) -> p h d", d=DH)
                if name == "dve":
                    cv.wait(eng, g, c)
                    tr.wait(eng, g - 1, c)
                    if c == 0:
                        rtd.wait(eng, s)
                    cos = RT[:, 2 * k, t:t + 1, :].to_broadcast([P, 8, DH])
                    tq = TQ[:, c, :].rearrange("p (h d) -> p h d", d=DH)
                    t1.inc(eng.tensor_tensor(tq, q3, cos, ALU.mult))
                    sq.wait(eng, g, c)
                    sm.wait(eng, g - 1, k)
                    ss.inc(eng.tensor_reduce(SS[:, c, :], SQ[c % 2][:, :].rearrange("p (h d) -> p h d", d=DH),
                                             AX.X, ALU.add))
                if name == "act":
                    cv.wait(eng, g, c)
                    if c >= 2:
                        ss.wait(eng, g, c - 2)
                    else:
                        ss.wait(eng, g - 1, 2 + c)
                    sq.inc(eng.activation(SQ[c % 2][:, :], QR[:, c, :], ACT.Square))
                if name == "pool":
                    cv.wait(eng, g, c)
                    if c >= 2:
                        ad.wait(eng, g, c - 2)
                    else:
                        ad.wait(eng, g - 1, 2 + c)
                    if c == 0:
                        rtp.wait(eng, s)
                    settle(eng)
                    o3 = T2[c % 2][:, :].rearrange("p (h d) -> p h d", d=DH)
                    for h in range(2):
                        sin = RT[:, 2 * k + 1, t:t + 1, h * 32:h * 32 + 32].to_broadcast([P, 8, 32])
                        i = eng.tensor_tensor(o3[:, :, h * 32:h * 32 + 32],
                                              q3[:, :, (1 - h) * 32:(2 - h) * 32], sin, ALU.mult)
                    t2.inc(i)

            def front_norms(name, eng, s, t, k):
                g = s * TPB + t
                if name == "dve":
                    ss.wait(eng, g, 2 * k + 1)
                    rn.wait(eng, g - 1, k)
                    sm.inc(eng.tensor_scalar(SM[:, 2 * k:2 * k + 2, :], SS[:, 2 * k:2 * k + 2, :], NORM2_EPS,
                                             None, ALU.max))
                if name == "pool":
                    sm.wait(eng, g, k)
                    qn.wait(eng, g - 1, 2 * k + 1)
                    rn.inc(eng.tensor_tensor(RN[:, 2 * k:2 * k + 2, :], SM[:, 2 * k:2 * k + 2, :],
                                             mhalf[:, 0:16].rearrange("p (c h) -> p c h", c=2), ALU.pow))

            def front_sum(name, eng, s, t, c):
                g = s * TPB + t
                if name == "dve":
                    t2.wait(eng, g, c)
                    t1.wait(eng, g, c)
                    ad.inc(eng.tensor_tensor(TQ[:, c, :], TQ[:, c, :], T2[c % 2][:, :], ALU.add))

            def front_scale(name, eng, s, t, c):
                g = s * TPB + t
                if name == "dve":
                    rn.wait(eng, g, c // 2)
                    ad.wait(eng, g, c)
                    tq = TQ[:, c, :].rearrange("p (h d) -> p h d", d=DH)
                    r = RN[:, c, :].rearrange("p (h a) -> p h a", a=1).to_broadcast([P, 8, DH])
                    qn.inc(eng.tensor_tensor(tq, tq, r, ALU.mult))

            def feature_major(name, eng, s, t, c):
                g = s * TPB + t
                tb = bank[5]
                if name == "pe":
                    qn.wait(eng, g, c)
                    if c == 0:
                        ke0.wait(eng, g - 1)
                        ke1.wait(eng, g - 1)
                        if t == 2:
                            hb.wait(eng, s - 1)
                        if t == 3:
                            he.wait(eng, s - 1)
                    elif c < 3:
                        qe.wait(eng, g, c - 1)
                    else:
                        ke0.wait(eng, g, 0)
                        ke1.wait(eng, g, 0)
                    for i in range(4):
                        m = eng.transpose(tb[:, i * P:(i + 1) * P], TQ[:, c, i * P:(i + 1) * P], ident[:, :])
                    tr.inc(m)
                v4 = tb[:, :].rearrange("p (i q) -> p i q", i=4)
                if name == "act":
                    tr.wait(eng, g, c)
                    scl.wait(eng, g - 1)
                    if c < 2:
                        qe.inc(eng.activation(QTL[:, 4 * c:4 * c + 4, :], v4, ACT.Copy))
                    else:
                        a = 4 * (c - 2)
                        ke1.inc(eng.activation(KZL[DH:P, a:a + 4, 1, WIN + t * P:WIN + (t + 1) * P],
                                               v4[DH:P, :, :], ACT.Copy))
                if name == "dve" and c >= 2:
                    tr.wait(eng, g, c)
                    scl.wait(eng, g - 1)
                    a = 4 * (c - 2)
                    ke0.inc(eng.tensor_copy(KZL[0:DH, a:a + 4, 0, WIN + t * P:WIN + (t + 1) * P], v4[0:DH, :, :]))

            def local_scores(name, eng, s, t, hg):
                g = s * TPB + t
                sbk = bank[2 + hg % 2]
                n = HG * SPAN
                if name == "pe":
                    if hg % 2 == 0:
                        qe.wait(eng, g, hg // 2)
                        ke0.wait(eng, g, hg // 2)
                        ke1.wait(eng, g, hg // 2)
                    if hg >= 2:
                        exl.wait(eng, g, hg - 2)
                    else:
                        exl.wait(eng, g - 1, 2 + hg)
                    eng.matmul(sbk[:, 0:n], identb[:, :], band[:, 0 if t == 0 else 1, :, :]
                               .rearrange("p h j -> p (h j)"), start=True, stop=False, skip_group_check=True)
                    for pl in range(2):
                        pr = 2 * hg + pl
                        for grp in range(2):
                            k0 = t * P + grp * GRP
                            m = eng.matmul(sbk[grp * GRP:(grp + 1) * GRP, pl * 2 * SPAN:(pl + 1) * 2 * SPAN],
                                           QTL[:, pr, grp * GRP:(grp + 1) * GRP], KZL[:, pr, :, k0:k0 + SPAN],
                                           start=False, stop=(pl == 1), skip_group_check=True)
                    scl.inc(m)

            def local_softmax(name, eng, s, t, hg):
                g = s * TPB + t
                s3 = bank[2 + hg % 2][:, 0:HG * SPAN].rearrange("p (h j) -> p h j", h=HG)
                pl = PL[hg % 2]
                cols = slice(HG * hg, HG * hg + HG)
                if name == "dve":
                    scl.wait(eng, g, hg)
                    exl.wait(eng, g - 1, hg)
                    nml.inc(eng.tensor_reduce(NML[:, cols], s3, AX.X, ALU.max, negate=True))
                if name == "act":
                    nml.wait(eng, g, hg)
                    ril.wait(eng, g - 1, hg)
                    if hg >= 2:
                        ptl.wait(eng, g, hg - 2)
                    else:
                        ptl.wait(eng, g - 1, 2 + hg)
                    for h in range(HG):
                        c = HG * hg + h
                        i = eng.activation(pl[:, h, :], s3[:, h, :], ACT.Exp, bias=NML[:, c:c + 1],
                                           accum_out=RSL[:, c:c + 1])
                    exl.inc(i)

            def local_normalise(name, eng, s, t, hg):
                g = s * TPB + t
                cols = slice(HG * hg, HG * hg + HG)
                if name == "dve":
                    exl.wait(eng, g, hg)
                    pnl.wait(eng, g - 1, hg)
                    ril.inc(eng.reciprocal(RIL[:, cols], RSL[:, cols]))
                    ril.wait(eng, g, hg)
                    pl = PL[hg % 2]
                    r = RIL[:, cols].rearrange("p (h a) -> p h a", a=1).to_broadcast([P, HG, SPAN])
                    pnl.inc(eng.tensor_tensor(pl[:, :, :], pl[:, :, :], r, ALU.mult))

            def local_transpose(name, eng, s, t, hg):
                g = s * TPB + t
                if name == "pe":
                    pnl.wait(eng, g, hg)
                    if hg:
                        pcl.wait(eng, g, hg - 1)
                    else:
                        pcl.wait(eng, g - 1)
                    for h in range(HG):
                        i = eng.transpose(bank[4][0:SPAN, h * P:(h + 1) * P], PL[hg % 2][:, h, :], ident[:, :])
                    ptl.inc(i)
                if name == "act":
                    ptl.wait(eng, g, hg)
                    if hg >= 2:
                        avl.wait(eng, g, hg - 2)
                    else:
                        avl.wait(eng, g - 1, 2 + hg)
                    pcl.inc(eng.activation(PTL[hg % 2][:, :], bank[4][0:SPAN, :], ACT.Copy))

            def local_av(name, eng, s, t, hg):
                g = s * TPB + t
                if name == "pe":
                    pcl.wait(eng, g, hg)
                    if hg == 0:
                        v_placed(eng, s, t)
                        ovl.wait(eng, g - 1)
                    if hg == 2:
                        ovl.wait(eng, g, 0)
                    for h in range(HG):
                        head = HG * hg + h
                        pl, e = divmod(head % 8, 2)
                        for grp in range(2):
                            o0 = pl * P + grp * GRP
                            i = eng.matmul(bank[6][e * DH:(e + 1) * DH, o0:o0 + GRP],
                                           VG[t % 2][:, grp, head * DH:(head + 1) * DH],
                                           PTL[hg % 2][:, h * P + grp * GRP:h * P + (grp + 1) * GRP],
                                           start=True, stop=True)
                    avl.inc(i)
                if name == "act" and hg % 2:
                    avl.wait(eng, g, hg)
                    yl.wait(eng, g - 1)
                    ovl.inc(eng.activation(OTL[:, 2 * hg - 2:2 * hg + 2, :],
                                           bank[6][:, :].rearrange("p (i q) -> p i q", i=4), ACT.Copy))

            def local_out(name, eng, s, t, half, nxt=True):
                g = s * TPB + t
                lp = (s // BATCH) % 2
                if name == "pe":
                    ovl.wait(eng, g, half)
                    if half == 0:
                        if t == 0:
                            gxt.wait(eng, s - 1)
                        elif t == 1:
                            hb.wait(eng, s - 1)
                        elif t == 2:
                            fin.wait(eng, s - 1)
                        if nxt:
                            fxd.wait(eng, g + 1)
                            fxa.wait(eng, g + 1)
                        else:
                            x2.wait(eng, g - 1)
                    for pr in range(4 * half, 4 * half + 4):
                        i = eng.matmul(bank[7][:, 0:E], OTL[:, pr, :], WO[:, lp, pr, :],
                                       start=(pr == 0), stop=(pr == PAIRS - 1))
                    if half:
                        yl.inc(i)
                if name == "dve" and half:
                    yl.wait(eng, g)
                    g1.wait(eng, s - 1)
                    x2b.wait(eng, g - TPB)
                    x2.inc(eng.tensor_tensor(X2[:, t, :], bank[7][:, 0:E], X[:, (s % BATCH) * TPB + t, :], ALU.add))

            def residual(name, eng, s, t):
                g = s * TPB + t
                lp = (s // BATCH) % 2
                if name == "pool":
                    x2.wait(eng, g)
                    fin.wait(eng, s - 2)
                    settle(eng)
                    x2b.inc(eng.tensor_tensor(X2B[:, s % 2, t, :], X2[:, t, :], B2[:, lp, :], ALU.add))

            m = bank[7]
            m3 = m[:, :].rearrange("p (t e) -> p t e", t=TPB)

            def ffn_turn(name, eng, s, alone=False):
                if name == "pe":
                    x2.wait(eng, s * TPB + TPB - 1)
                    if not alone:
                        fxd.wait(eng, (s + 1) * TPB + 1)
                        fxa.wait(eng, (s + 1) * TPB + 1)
                    for t in range(TPB):
                        i = eng.transpose(m[:, t * P:(t + 1) * P], X2[:, t, :], ident[:, :])
                    g1.inc(i)
                if name == "dve":
                    g1.wait(eng, s)
                    g2.wait(eng, s - 1)
                    g1d.inc(eng.tensor_copy(XT2[0:DH, 0:SEQ], m[0:DH, :]))
                if name == "act":
                    g1.wait(eng, s)
                    g2.wait(eng, s - 1)
                    g1a.inc(eng.activation(XT2[DH:P, 1:SEQ + 1], m[DH:P, :], ACT.Copy))

            def ffn_norm(name, eng, s):
                if name == "pe":
                    g1d.wait(eng, s)
                    g1a.wait(eng, s)
                    for t in range(TPB):
                        i = eng.transpose(m[:, t * P:(t + 1) * P], XT2[:, t * P:(t + 1) * P], ident[:, :])
                    g2.inc(i)
                if name == "dve":
                    g2.wait(eng, s)
                    for t in range(TPB):
                        gst.inc(eng.bn_stats(stats[:, t, :], m3[:, t, :]))
                    gst.wait(eng, s, TPB - 1)
                    settle(eng)
                    for t in range(TPB):
                        i = eng.bn_aggr(mv[:, t, :], stats[:, t, :])
                    gst.inc(i)
                    gst.wait(eng, s)
                    gve.inc(eng.tensor_scalar(veps[:, :], mv[:, :, 1], LN_EPS, None, ALU.add))
                if name == "pool":
                    gve.wait(eng, s)
                    gxn.wait(eng, s - 1)
                    grs.inc(eng.tensor_tensor(rstd[:, :], veps[:, :], mhalf[:, 0:TPB], ALU.pow))

            def ffn_norm2(name, eng, s):
                if name == "dve":
                    grs.wait(eng, s)
                    g3.wait(eng, s - 1)
                    for t in range(TPB):
                        i = eng.tensor_scalar(XN[:, t, :], m3[:, t, :], mv[:, t, 0:1], rstd[:, t:t + 1],
                                              ALU.subtract, ALU.mult)
                    gxn.inc(i)

            def ffn_gain(name, eng, s):
                if name == "pe":
                    gxn.wait(eng, s)
                    for t in range(TPB):
                        i = eng.transpose(m[:, t * P:(t + 1) * P], XN[:, t, :], ident[:, :])
                    g3.inc(i)
                if name == "act":
                    g3.wait(eng, s)
                    hh.wait(eng, s - 1)
                    gsel = GBA[:, 0, bass.ds(s // BATCH, 1)]
                    bsel = GBA[:, 1, bass.ds(s // BATCH, 1)]
                    gxt.inc(eng.activation(XNT2[:, :], m[:, :], ACT.Identity, scale=gsel, bias=bsel))

            def ffn_up(name, eng, s, t):
                lp = (s // BATCH) % 2
                up = (bank[5], bank[7])
                dst = (A1, G1)
                if name == "pe":
                    gxt.wait(eng, s)
                    if t == 0:
                        later = not isinstance(s, int) or s < STEPS - 1
                        ke0.wait(eng, (s + 1) * TPB + 1 if later else s * TPB + TPB - 1)
                        ke1.wait(eng, (s + 1) * TPB + 1 if later else s * TPB + TPB - 1)
                        if later:
                            fxd.wait(eng, (s + 1) * TPB + 2)
                            fxa.wait(eng, (s + 1) * TPB + 2)
                    for k in range(2):
                        if t:
                            hb.wait(eng, s, 2 * (t - 1) + k)
                        hh.inc(eng.matmul(up[k][:, 0:FF], XNT2[:, t * P:(t + 1) * P],
                                          W1[:, lp, k * FF:(k + 1) * FF], start=True, stop=True))
                if name == "dve":
                    for k in range(2):
                        hh.wait(eng, s, 2 * t + k)
                        if k == 0:
                            ht.wait(eng, s - 1)
                        else:
                            hm.wait(eng, s - 1)
                        hb.inc(eng.tensor_tensor(dst[k][:, t, :], up[k][:, 0:FF],
                                                 B1[:, lp, k * FF:(k + 1) * FF], ALU.add))

            def ffn_gelu(name, eng, s):
                if name == "act":
                    hb.wait(eng, s)
                    ge.inc(eng.activation(G1[:, :, :], G1[:, :, :], ACT.Gelu))
                if name == "pool":
                    ge.wait(eng, s)
                    for t in range(TPB):
                        hm.inc(eng.tensor_tensor(A1[:, t, :], A1[:, t, :], G1[:, t, :], ALU.mult))

            def ffn_turn_h(name, eng, s, t):
                tb = bank[5]
                if name == "pe":
                    hm.wait(eng, s, t)
                    if t:
                        he.wait(eng, s, t - 1)
                    else:
                        later = not isinstance(s, int) or s < STEPS - 1
                        if later:
                            ke0.wait(eng, (s + 1) * TPB + 2)
                            ke1.wait(eng, (s + 1) * TPB + 2)
                        hb.wait(eng, s)
                    for c, (c0, n) in enumerate(FFC):
                        i = eng.transpose(tb[0:n, c * P:(c + 1) * P], A1[:, t, c0:c0 + n], ident[:, :])
                    ht.inc(i)
                if name == "act":
                    ht.wait(eng, s, t)
                    if t >= 2:
                        fy.wait(eng, s, t - 2)
                    else:
                        fy.wait(eng, s - 1, 2 + t)
                    nf = len(FFC) - 1
                    n = FFC[nf][1]
                    eng.activation(HT[t % 2][:, 0:nf, :], tb[:, 0:nf * P].rearrange("p (c q) -> p c q", c=nf),
                                   ACT.Copy)
                    he.inc(eng.activation(HT[t % 2][0:n, nf, :], tb[0:n, nf * P:(nf + 1) * P], ACT.Copy))

            def ffn_down(name, eng, s, t):
                lp = (s // BATCH) % 2
                if name == "pe":
                    he.wait(eng, s, t)
                    if t:
                        fin.wait(eng, s, t - 1)
                    else:
                        later = not isinstance(s, int) or s < STEPS - 1
                        if later:
                            fxd.wait(eng, (s + 1) * TPB + 3)
                            fxa.wait(eng, (s + 1) * TPB + 3)
                    for c, (c0, n) in enumerate(FFC):
                        i = eng.matmul(m[:, 0:E], HT[t % 2][0:n, c, :], W2[0:n, lp, c, :],
                                       start=(c == 0), stop=(c == len(FFC) - 1))
                    fy.inc(i)
                if name == "dve":
                    fy.wait(eng, s, t)
                    x2b.wait(eng, s * TPB + t)
                    fin.inc(eng.tensor_tensor(X[:, (s % BATCH) * TPB + t, :], m[:, 0:E],
                                              X2B[:, s % 2, t, :], ALU.add))

            def ffn_alone(name, eng, s):
                residual(name, eng, s, TPB - 1)
                ffn_turn(name, eng, s, alone=True)
                ffn_norm(name, eng, s)
                ffn_norm2(name, eng, s)
                ffn_gain(name, eng, s)
                for t in range(TPB):
                    ffn_up(name, eng, s, t)
                ffn_gelu(name, eng, s)
                for t in range(TPB):
                    ffn_turn_h(name, eng, s, t)
                    ffn_down(name, eng, s, t)

            def slot(name, eng, s, t, nxt=True, with_ffn=True, first=False):
                fs, ft = (s, t + 1) if t < TPB - 1 else (s + 1, 0)
                a = (name, eng, s, t)

                def front(c):
                    if nxt:
                        front_chunk(name, eng, fs, ft, c)

                def rot_a(c):
                    if nxt:
                        front_products(name, eng, fs, ft, c)

                def norms(k):
                    if nxt:
                        front_norms(name, eng, fs, ft, k)

                def rot_b(c):
                    if nxt:
                        front_sum(name, eng, fs, ft, c)

                def rot_c(c):
                    if nxt:
                        front_scale(name, eng, fs, ft, c)

                def beside(*stages):
                    if with_ffn and t < len(stages) and stages[t]:
                        for f in stages[t]:
                            f(name, eng, s - 1)

                def up(i):
                    return lambda n, e, b: ffn_up(n, e, b, i)

                def turn_h(i):
                    return lambda n, e, b: ffn_turn_h(n, e, b, i)

                def down(i):
                    return lambda n, e, b: ffn_down(n, e, b, i)

                if nxt and ft == 0:
                    rotary_tables(name, eng, fs)
                feature_major(*a, 0)
                if nxt:
                    front_x(name, eng, fs, ft)
                if not first:
                    residual(name, eng, *((s, t - 1) if t else (s - 1, TPB - 1)))
                feature_major(*a, 1)
                front(0)
                feature_major(*a, 2)
                front(1)
                beside([ffn_turn])
                local_scores(*a, 0)
                local_softmax(*a, 0)
                feature_major(*a, 3)
                rot_a(0)
                front(2)
                beside([ffn_norm], [up(0)], [turn_h(0)])
                local_scores(*a, 1)
                local_softmax(*a, 1)
                local_normalise(*a, 0)
                rot_a(1)
                rot_b(0)
                norms(0)
                beside([ffn_norm2], [up(1)], [down(0), turn_h(1)])
                local_transpose(*a, 0)
                front(3)
                local_scores(*a, 2)
                local_softmax(*a, 2)
                local_normalise(*a, 1)
                rot_a(2)
                rot_b(1)
                local_av(*a, 0)
                beside([ffn_gain], [up(2)], [down(1), turn_h(2)])
                local_transpose(*a, 1)
                front(4)
                local_scores(*a, 3)
                local_softmax(*a, 3)
                local_normalise(*a, 2)
                rot_a(3)
                rot_b(2)
                rot_c(0)
                norms(1)
                local_av(*a, 1)
                beside([], [up(3), ffn_gelu], [down(2), turn_h(3)])
                local_transpose(*a, 2)
                local_normalise(*a, 3)
                rot_b(3)
                rot_c(1)
                front(5)
                if nxt:
                    place_v(name, eng, fs, ft)
                local_av(*a, 2)
                beside([], [], [down(3)])
                local_transpose(*a, 3)
                local_out(*a, 0, nxt)
                rot_c(2)
                rot_c(3)
                local_av(*a, 3)
                local_out(*a, 1, nxt)

            def layers_program(name, eng):
                if name == "sp":
                    in_dma(eng, s_i, ROT[:, :, :, :], rot.rearrange("k (t p) d -> p k t d", p=P))
                    in_dma(eng, s_i, LGB[0:DEPTH, :], lng)
                    in_dma(eng, s_i, LGB[DEPTH:2 * DEPTH, :], lnb)
                    for i in range(2):
                        eng.sem_inc(s_v[i], 48)
                    load_layer(eng, 0, 0, s_w)
                    eng.wait_ge(s_k, 11)

                    def steps_v(first, n):
                        with eng.Fori(0, n) as i:
                            for t in range(TPB):
                                place_v(name, eng, first + i, t)

                    with eng.Fori(0, DEPTH - 1) as l:
                        for t in range(TPB):
                            place_v(name, eng, l * BATCH, t)
                        fin.wait(eng, l * BATCH - 1)
                        rtd.wait(eng, l * BATCH)
                        eng.wait_ge(s_w, (l + 1) * 16 * NW)
                        load_layer(eng, bass.ds(l + 1, 1), (l + 1) % 2, s_w)
                        steps_v(l * BATCH + 1, BATCH - 1)
                    steps_v((DEPTH - 1) * BATCH, BATCH)
                    eng.wait_ge(s_w, DEPTH * 16 * NW)
                    eng.wait_ge(s_i, 48)
                    for t in (TPB - 2, TPB - 1):
                        v_placed(eng, STEPS - 1, t)
                    return
                if name == "pool":
                    eng.memset(KZL[:, :, :, :], 0.0).then_inc(s_k, 1)
                    eng.memset(XT[:, :], 0.0).then_inc(s_k, 1)
                    eng.memset(XT2[:, :], 0.0).then_inc(s_k, 1)
                    eng.memset(band[:, :, :, :], 0.0).then_inc(s_k, 1)
                    eng.memset(none[:, :], 0.0).then_inc(s_k, 1)
                    eng.memset(VN[1][:, :], 0.0).then_inc(s_k, 1)
                    eng.wait_ge(s_k, 6)
                    n = 0
                    for grp in range(2):
                        rows = slice(grp * GRP, (grp + 1) * GRP)
                        bm = band[rows, :, :, :].rearrange("p k h j -> p (k h) j")
                        eng.affine_select(out=bm, in_=bm, compare_op=ALU.is_ge, fill=FORBID, base=0,
                                          pattern=[[0, 2 * HG], [1, SPAN]], channel_multiplier=-1).then_inc(s_k, 1)
                        n += 1
                        eng.wait_ge(s_k, 6 + n)
                        eng.affine_select(out=bm, in_=bm, compare_op=ALU.is_ge, fill=FORBID, base=WIN,
                                          pattern=[[0, 2 * HG], [-1, SPAN]], channel_multiplier=1).then_inc(s_k, 1)
                        n += 1
                        eng.wait_ge(s_k, 6 + n)
                    eng.memset(band[0:GRP, 0, :, 0:WIN], FORBID).then_inc(s_k, 1)
                if name == "dve":
                    i = eng.tensor_copy(XM[:, :, :], X[:, :, :])
                    i.then_inc(s_m, 1)
                    eng.wait_ge(s_m, 1)
                with_ln = ln2
                if name in ("dve", "pool"):
                    with eng.Fori(0, BATCH) as b:
                        with_ln(name, eng, b)
                if name == "pool":
                    lx.wait(eng, BATCH - 1)
                if name != "sp":
                    eng.wait_ge(s_k, 11)
                    eng.wait_ge(s_i, 48)
                ln_gains(name, eng)
                rotary_tables(name, eng, 0)
                front_x(name, eng, 0, 0)
                for c in range(6):
                    front_chunk(name, eng, 0, 0, c)
                for k in range(2):
                    for c in (2 * k, 2 * k + 1):
                        front_products(name, eng, 0, 0, c)
                        front_sum(name, eng, 0, 0, c)
                    front_norms(name, eng, 0, 0, k)
                    for c in (2 * k, 2 * k + 1):
                        front_scale(name, eng, 0, 0, c)
                for t in range(TPB - 1):
                    slot(name, eng, 0, t, with_ffn=False, first=(t == 0))
                with eng.Fori(0, STEPS - 1) as s:
                    slot(name, eng, s, TPB - 1)
                    for t in range(TPB - 1):
                        slot(name, eng, s + 1, t)
                slot(name, eng, STEPS - 1, TPB - 1, nxt=False)
                ffn_alone(name, eng, STEPS - 1)

            lst = sig("lst", 5, "dve")
            lve = sig("lve", 1, "dve")
            lrs = sig("lrs", 1, "pool")
            lx = sig("lx", 4, "dve")

            def ln2(name, eng, b):
                if name == "dve":
                    for t in range(TPB):
                        lst.inc(eng.bn_stats(stats[:, t, :], X[:, b * TPB + t, :]))
                    lst.wait(eng, b, TPB - 1)
                    settle(eng)
                    for t in range(TPB):
                        i = eng.bn_aggr(mv[:, t, :], stats[:, t, :])
                    lst.inc(i)
                    lst.wait(eng, b)
                    lrs.wait(eng, b - 1)
                    lve.inc(eng.tensor_scalar(veps[:, :], mv[:, :, 1], LN_EPS, None, ALU.add))
                    lrs.wait(eng, b)
                    for t in range(TPB):
                        xt = X[:, b * TPB + t, :]
                        lx.inc(eng.tensor_scalar(xt, xt, mv[:, t, 0:1], rstd[:, t:t + 1],
                                                 ALU.subtract, ALU.mult))
                if name == "pool":
                    lve.wait(eng, b)
                    lx.wait(eng, b - 1)
                    lrs.inc(eng.tensor_tensor(rstd[:, :], veps[:, :], mhalf[:, 0:TPB], ALU.pow))

            engines_run(nc, sigs, layers_program)

        with ExitStack() as ctx:
            s_o = ctx.enter_context(nc.semaphore("s_o"))
            s_d = ctx.enter_context(nc.semaphore("s_d"))

            def out_program(name, eng):
                for b in range(BATCH):
                    r = slice(b * TPB, (b + 1) * TPB)
                    if name == "dve":
                        eng.tensor_tensor(XM[:, r, :], XM[:, r, :], X[:, r, :], ALU.add).then_inc(s_o, 1)
                    if name == "sp":
                        eng.wait_ge(s_o, b + 1)
                        eng.dma_start(out_t[:, r, :], XM[:, r, :]).then_inc(s_d, 16)
                if name == "sp":
                    eng.wait_ge(s_d, 16 * BATCH)

            engines_run(nc, (), out_program)


_INS = ['L0_attn_x', 'L0_attn_Wq', 'L0_attn_Wk', 'L0_attn_Wv', 'L0_attn_Wr', 'L0_ffn_Wqkv', 'L0_ffn_q_scale',
        'L0_ffn_k_scale', 'L0_ffn_Wo', 'L0_ffn_ln_g', 'L0_ffn_ln_b', 'L0_ffn_W1', 'L0_ffn_b1', 'L0_ffn_W2',
        'L0_ffn_b2']


def rotary_constants():
    import numpy as np
    f = np.float32
    half = np.arange(0, DH, 2, dtype=f)
    inv_freq = (f(1.0) / np.power(f(10000.0), half / f(DH))).astype(f)
    pos = np.arange(SEQ, dtype=f)
    freqs = (pos[:, None] * inv_freq[None, :]).astype(f)
    freqs = np.concatenate([freqs, freqs], -1).astype(np.float64)
    base = ((half + f(0.4 * DH)) / f(1.4 * DH)).astype(f)
    power = ((pos - SEQ // 2) / f(WIN // 2)).astype(f)
    scale = np.power(base[None, :].astype(np.float64), power[:, None])
    scale = np.concatenate([scale, scale], -1)
    sign = np.where(np.arange(DH) < DH // 2, -1.0, 1.0)
    cos, sin = np.cos(freqs), np.sin(freqs) * sign
    return np.stack([cos * scale * QK_SCALE, sin * scale * QK_SCALE, cos / scale, sin / scale]).astype(f)


def kernel(**inputs):
    import numpy as _np
    import concourse.bacc as _bacc
    from concourse import mybir as _mybir
    from concourse.bass_utils import run_bass_kernel_spmd as _run

    nc = _bacc.Bacc("TRN2", target_bir_lowering=False, num_devices=1)
    arrays, args = {}, []
    for name in _INS:
        arrays[f"in_{name}_dram"] = _np.ascontiguousarray(inputs[name])
    arrays["rotary_dram"] = rotary_constants()
    for name, a in arrays.items():
        args.append(nc.dram_tensor(name, a.shape, _mybir.dt.from_np(a.dtype), kind="ExternalInput").ap())
    args.append(nc.dram_tensor("out_0_dram", (BATCH, SEQ, E), F32, kind="ExternalOutput").ap())
    build(nc, *args)
    r = _run(nc, [arrays], core_ids=[0])
    return r.results[0]["out_0_dram"]
```

```python
from contextlib import ExitStack

import concourse.bass as bass
from concourse import mybir

F32 = mybir.dt.float32
BF16 = mybir.dt.bfloat16
ALU = mybir.AluOpType
ACT = mybir.ActivationFunctionType
AX = mybir.AxisListType

P = 128
E = 128
HEADS = 16
DH = 64
INNER = HEADS * DH
PAIRS = HEADS // 2
BATCH = 4
SEQ = 512
TPB = SEQ // P
TILES = BATCH * TPB
DEPTH = 6
WIN = 32
GRP = 2 * WIN
SPAN = GRP + WIN
HG = 4
NHG = HEADS // HG
FF = int(E * 4 * 2 / 3)
FFC = [(c, min(P, FF - c)) for c in range(0, FF, P)]
STEPS = DEPTH * BATCH
PENALTY = -50.0
FORBID = -1e25
SCALE = 0.125
QK_SCALE = 8.0
LN_EPS = 1e-5
NORM2_EPS = 1e-24
UP_FIRST = 2


ORDER = {
    "pe": (
        "turn_qk0 ~turn_p3 ~av2 turn_qk1 ~av3 ~out0 turn_qk2 ~out1 score0 x score1 turn_qk3 "
        "chunk0 chunk1 0:turn 3:turn_h0 1:up0 chunk2 score2 3:down0 3:turn_h1 0:stat turn_p0 "
        "chunk3 3:turn_h2 score3 turn_p1 2:up2 2:up3 3:turn_h3 3:down1 1:up1 chunk4 3:down2 av0 "
        "av1 3:down3 0:gain turn_p2 chunk5"),
    "act": (
        "turn_qk0 ~turn_p3 ~chunk4 turn_qk1 ~av3 ~chunk5 stage_x turn_qk2 x exp0 turn_qk3 chunk0 "
        "chunk1 sq0 3:turn_h0 sq1 0:turn exp1 3:turn_h1 chunk2 turn_p0 3:turn_h2 chunk3 exp2 "
        "turn_p1 sq2 3:turn_h3 sq3 exp3 2:gelu 0:gain turn_p2 av1"),
    "dve": (
        "tables turn_qk2 ~sum3 ~out1 ~scale3 max0 x turn_qk3 max1 recip0 div0 rot0 rot1 sq0 sq1 "
        "0:turn pow0 sum0 recip1 max2 3:down0 0:stat div1 1:up0 3:down1 sum1 max3 2:up2 3:down2 "
        "recip2 0:norm 2:up3 div2 sq2 sq3 1:up1 pow1 recip3 div3 3:down3 rot2 rot3 sum2 scale2"),
    "pool": (
        "tables rot0 rot1 pow0 0:stat scale0 rot2 scale1 pow1 ~resid rot3 2:gelu"),
}


class Sig:

    def __init__(self, nc, ctx, name, per, owner, lag=1):
        self.sem = ctx.enter_context(nc.semaphore(name))
        self.per, self.owner, self.lag = per, owner, lag

    def start(self, engine):
        engine.sem_inc(self.sem, self.lag * self.per)

    def inc(self, ins):
        ins.then_inc(self.sem, 1)

    def wait(self, engine, unit, event=None):
        n = self.per - 1 if event is None else event
        engine.wait_ge(self.sem, (unit + self.lag) * self.per + n + 1)


def engines_run(nc, sigs, program):
    with nc.Block() as block:
        for name, deco in (("pe", block.tensor), ("act", block.scalar), ("dve", block.vector),
                           ("pool", block.gpsimd), ("sp", block.sync)):
            def body(eng, name=name):
                for s in sigs:
                    if s.owner == name:
                        s.start(eng)
                program(name, eng)
            deco(body)


def build(nc, x, wq, wk, wv, wr, wqkv, qscale, kscale, wo, lng, lnb, w1, b1, w2, b2, rot, out):
    with ExitStack() as keep:
        def sb(name, shape, dt=F32, ctx=keep):
            return ctx.enter_context(nc.sbuf_tensor(name, shape, dt))

        bank = [keep.enter_context(nc.psum_tensor(f"bank{i}", [P, 512], F32)) for i in range(8)]
        X = sb("X", [P, TILES, E])
        XM = sb("XM", [P, TILES, E])
        ident = sb("ident", [P, P])
        s_c = keep.enter_context(nc.semaphore("s_const"))

        passed = {}

        def settle(eng):
            k = str(eng.engine)
            if k not in passed:
                passed[k] = keep.enter_context(nc.semaphore(f"passed{len(passed)}"))
            eng.sem_inc(passed[k], 1)

        identb = sb("identb", [P, P], BF16)
        stats = sb("stats", [P, TPB, 6])
        mv = sb("mv", [P, TPB, 2])
        veps = sb("veps", [P, TPB])
        rstd = sb("rstd", [P, TPB])
        mhalf = sb("mhalf", [P, 64])

        def in_dma(engine, sem, dst, src):
            engine.dma_start(dst, src).then_inc(sem, 16)

        x_t = x.rearrange("b (t p) e -> p (b t) e", p=P)
        out_t = out.rearrange("b (t p) e -> p (b t) e", p=P)

        band = sb("band", [P, 2, HG, SPAN], BF16)
        XT = sb("XT", [P, SEQ + 1])
        XT2 = sb("XT2", [P, SEQ + 1])
        VN = [sb(f"VN{i}", [P, INNER]) for i in range(2)]
        none = sb("none", [WIN, INNER])
        KZL = sb("KZL", [P, PAIRS, 2, WIN + SEQ])
        s_k = keep.enter_context(nc.semaphore("s_k"))

        def clear_and_mask(eng):
            eng.memset(KZL[:, :, :, :], 0.0).then_inc(s_k, 1)
            eng.memset(XT[:, :], 0.0).then_inc(s_k, 1)
            eng.memset(XT2[:, :], 0.0).then_inc(s_k, 1)
            eng.memset(band[:, :, :, :], 0.0).then_inc(s_k, 1)
            eng.memset(none[:, :], 0.0).then_inc(s_k, 1)
            eng.memset(VN[1][:, :], 0.0).then_inc(s_k, 1)
            eng.wait_ge(s_k, 6)
            n = 6
            for grp in range(2):
                rows = slice(grp * GRP, (grp + 1) * GRP)
                bm = band[rows, :, :, :].rearrange("p k h j -> p (k h) j")
                for base, sign in ((0, 1), (WIN, -1)):
                    eng.affine_select(out=bm, in_=bm, compare_op=ALU.is_ge, fill=FORBID, base=base,
                                      pattern=[[0, 2 * HG], [sign, SPAN]],
                                      channel_multiplier=-sign).then_inc(s_k, 1)
                    n += 1
                    eng.wait_ge(s_k, n)
            eng.memset(band[0:GRP, 0, :, 0:WIN], FORBID).then_inc(s_k, 1)

        with ExitStack() as ctx:
            def sbl(name, shape, dt=F32):
                return sb(name, shape, dt, ctx)

            W0 = sbl("W0", [P, 3, INNER])
            WR = sbl("WR", [P, PAIRS, E])
            XNT = sbl("XNT", [P, BATCH * SEQ])
            XN0 = sbl("XN0", [P, TPB, E])
            WP = [sbl(f"WP{i}", [P, 3, P]) for i in range(2)]
            XNS = [sbl(f"XNS{i}", [P, SEQ]) for i in range(2)]
            QT = [sbl(f"QT{i}", [P, SEQ]) for i in range(2)]
            KZ = [sbl(f"KZ{i}", [P, 2, SEQ]) for i in range(2)]
            V = [sbl(f"V{i}", [P, TPB, P]) for i in range(2)]
            PR = [sbl(f"PR{i}", [P, SEQ]) for i in range(2)]
            PTS = [[sbl(f"PTS{i}{e}", [P, TPB, SEQ]) for e in range(2)] for i in range(2)]
            OT = sbl("OT", [P, SEQ])
            NM = sbl("NM", [P, 8])
            RS = sbl("RS", [P, 8])
            RI = sbl("RI", [P, 8])
            causal = sbl("causal", [P, SEQ], BF16)

            s_in = ctx.enter_context(nc.semaphore("s_x"))
            s_w0 = ctx.enter_context(nc.semaphore("s_w0"))
            lnst = Sig(nc, ctx, "lnst", 5, "dve")
            lnve = Sig(nc, ctx, "lnve", 1, "dve")
            lnrs = Sig(nc, ctx, "lnrs", 1, "pool")
            lnxn = Sig(nc, ctx, "lnxn", 4, "dve")
            lntr = Sig(nc, ctx, "lntr", 1, "pe")
            lnev = Sig(nc, ctx, "lnev", 1, "act")

            def ln_program(name, eng):
                if name == "sp":
                    for i in range(2):
                        in_dma(eng, s_in, X[:, 8 * i:8 * i + 8, :], x_t[:, 8 * i:8 * i + 8, :])
                    for i, w in enumerate((wq, wk, wv)):
                        in_dma(eng, s_w0, W0[:, i, :], w)
                    in_dma(eng, s_w0, WR[:, :, :], wr.rearrange("(c p) e -> p c e", p=P))
                    eng.wait_ge(s_w0, 64)
                if name == "pool":
                    eng.memset(ident[:, :], 0.0).then_inc(s_c, 1)
                    eng.memset(identb[:, :], 0.0).then_inc(s_c, 1)
                    eng.memset(causal[:, :], 0.0).then_inc(s_c, 1)
                    eng.memset(mhalf[:, :], -0.5).then_inc(s_c, 1)
                    for i in range(2):
                        eng.memset(KZ[i][:, :, :], 0.0).then_inc(s_c, 1)
                    eng.wait_ge(s_c, 6)
                    for m in (ident, identb):
                        eng.affine_select(out=m[:, :], in_=m[:, :], compare_op=ALU.not_equal, fill=1.0,
                                          base=0, pattern=[[-1, P]], channel_multiplier=1).then_inc(s_c, 1)
                    eng.affine_select(out=causal[:, :], in_=causal[:, :], compare_op=ALU.is_ge,
                                      fill=PENALTY, base=0, pattern=[[-1, SEQ]],
                                      channel_multiplier=1).then_inc(s_c, 1)
                if name == "sp":
                    return
                with eng.Fori(0, BATCH) as b:
                    if name == "dve":
                        eng.wait_ge(s_in, 32)
                        for t in range(TPB):
                            lnst.inc(eng.bn_stats(stats[:, t, :], X[:, b * TPB + t, :]))
                        for t in range(TPB):
                            lnst.wait(eng, b, t)
                            settle(eng)
                            i = eng.bn_aggr(mv[:, t, :], stats[:, t, :])
                        lnst.inc(i)
                        lnst.wait(eng, b)
                        lnrs.wait(eng, b - 1)
                        lnve.inc(eng.tensor_scalar(veps[:, :], mv[:, :, 1], LN_EPS, None, ALU.add))
                        lnrs.wait(eng, b)
                        lntr.wait(eng, b - 1)
                        for t in range(TPB):
                            lnxn.inc(eng.tensor_scalar(XN0[:, t, :], X[:, b * TPB + t, :], mv[:, t, 0:1],
                                                       rstd[:, t:t + 1], ALU.subtract, ALU.mult))
                    if name == "pool":
                        eng.wait_ge(s_c, 9)
                        lnve.wait(eng, b)
                        lnrs.inc(eng.tensor_tensor(rstd[:, :], veps[:, :], mhalf[:, 0:TPB], ALU.pow))
                    if name == "pe":
                        eng.wait_ge(s_c, 9)
                        lnxn.wait(eng, b)
                        lnev.wait(eng, b - 1)
                        for t in range(TPB):
                            i = eng.transpose(bank[7][:, t * P:(t + 1) * P], XN0[:, t, :], ident[:, :])
                        lntr.inc(i)
                    if name == "act":
                        lntr.wait(eng, b)
                        lnev.inc(eng.activation(XNT[:, bass.ds(b * SEQ, SEQ)], bank[7][:, :], ACT.Copy))

            engines_run(nc, (lnst, lnve, lnrs, lnxn, lntr, lnev), ln_program)

            NJ = 2 * TPB
            wps = Sig(nc, ctx, "wps", 2, "pool")
            pj = Sig(nc, ctx, "pj", 3, "pe")
            pja = Sig(nc, ctx, "pja", 3, "act")
            pjd = Sig(nc, ctx, "pjd", 1, "dve")
            sc = Sig(nc, ctx, "sc", NJ, "pe", 2)
            nm = Sig(nc, ctx, "nm", NJ, "dve")
            ex = Sig(nc, ctx, "ex", NJ, "act")
            ri = Sig(nc, ctx, "ri", NJ, "dve")
            pn = Sig(nc, ctx, "pn", NJ, "dve")
            pt = Sig(nc, ctx, "pt", NJ, "pe")
            pe = [Sig(nc, ctx, f"ptc{e}", TPB, own) for e, own in enumerate(("dve", "act"))]
            av = Sig(nc, ctx, "av", 1, "pe", 2)
            ov = Sig(nc, ctx, "ov", 1, "act")
            yy = Sig(nc, ctx, "yy", 1, "pe")
            xa = Sig(nc, ctx, "xa", 1, "dve")
            sigs0 = (wps, pj, pja, pjd, sc, nm, ex, ri, pn, pt, *pe, av, ov, yy, xa)

            def stage(name, eng, u, par):
                if name == "pool":
                    pj.wait(eng, u - 1)
                    w = eng.tensor_copy(WP[par][:, :, :], W0[:, :, bass.ds((u % PAIRS) * P, P)])
                    wps.inc(w)
                    wps.inc(eng.tensor_copy(XNS[par][:, :], XNT[:, bass.ds((u // PAIRS) * SEQ, SEQ)]))

            def project(name, eng, u, par, c):
                pb = bank[c % 2]
                if name == "pe":
                    wps.wait(eng, u)
                    if c == 0:
                        pja.wait(eng, u - 1, 2)
                        eng.matmul(pb[:, :], WP[par][:, 0, :], XNS[par][:, :], start=True, stop=True)\
                           .then_inc(pj.sem, 1)
                    if c == 1:
                        pja.wait(eng, u - 1, 1)
                        pjd.wait(eng, u - 1)
                        eng.matmul(pb[:, :], WP[par][:, 1, :], XNS[par][:, :], start=True, stop=True)\
                           .then_inc(pj.sem, 1)
                    if c == 2:
                        pja.wait(eng, u, 0)
                        for t in range(TPB):
                            i = eng.matmul(pb[:, t * P:(t + 1) * P], XNS[par][:, t * P:(t + 1) * P],
                                           WP[par][:, 2, :], start=True, stop=True)
                        pj.inc(i)
                if name == "act":
                    pj.wait(eng, u, c)
                    if c == 0:
                        sc.wait(eng, u - 2)
                        pja.inc(eng.activation(QT[par][:, :], pb[:, :], ACT.Copy))
                    if c == 1:
                        pja.inc(eng.activation(KZ[par][DH:P, 1, :], pb[DH:P, :], ACT.Copy, scale=SCALE))
                    if c == 2:
                        av.wait(eng, u - 2)
                        pja.inc(eng.activation(V[par][:, :, :], pb[:, :].rearrange("p (t d) -> p t d", t=TPB),
                                               ACT.Copy))
                if name == "dve" and c == 1:
                    pj.wait(eng, u, 1)
                    sc.wait(eng, u - 2)
                    pjd.inc(eng.tensor_scalar(KZ[par][0:DH, 0, :], pb[0:DH, :], SCALE, None, ALU.mult))

            def scores(name, eng, u, par, j):
                qt, e = divmod(j, 2)
                sbk = bank[2 + j % 2]
                if name == "pe":
                    pja.wait(eng, u, 1)
                    pjd.wait(eng, u)
                    if j >= 2:
                        ex.wait(eng, u, j - 2)
                    else:
                        ex.wait(eng, u - 1, NJ - 2 + j)
                    eng.matmul(sbk[:, :], QT[par][:, qt * P:(qt + 1) * P], KZ[par][:, e, :],
                               start=True, stop=False, skip_group_check=True)
                    sc.inc(eng.matmul(sbk[:, qt * P:SEQ], identb[:, :], causal[:, 0:SEQ - qt * P],
                                      start=False, stop=True, skip_group_check=True))

            def softmax(name, eng, u, par, j):
                sbk = bank[2 + j % 2]
                if name == "dve":
                    sc.wait(eng, u, j)
                    ex.wait(eng, u - 1, j)
                    nm.inc(eng.tensor_reduce(NM[:, j:j + 1], sbk[:, :], AX.X, ALU.max, negate=True))
                if name == "act":
                    nm.wait(eng, u, j)
                    ri.wait(eng, u - 1, j)
                    if j >= 2:
                        pt.wait(eng, u, j - 2)
                    else:
                        pt.wait(eng, u - 1, NJ - 2 + j)
                    ex.inc(eng.activation(PR[j % 2][:, :], sbk[:, :], ACT.Exp, bias=NM[:, j:j + 1],
                                          accum_out=RS[:, j:j + 1]))

            def normalise(name, eng, u, par, j):
                if name == "dve":
                    ex.wait(eng, u, j)
                    pn.wait(eng, u - 1, j)
                    ri.inc(eng.reciprocal(RI[:, j:j + 1], RS[:, j:j + 1]))
                    ri.wait(eng, u, j)
                    pn.inc(eng.tensor_scalar(PR[j % 2][:, :], PR[j % 2][:, :], RI[:, j:j + 1], None, ALU.mult))

            def transpose_p(name, eng, u, par, j):
                qt, e = divmod(j, 2)
                tb = bank[4 + j % 2]
                if name == "pe":
                    pn.wait(eng, u, j)
                    if qt:
                        pe[e].wait(eng, u, qt - 1)
                    else:
                        pe[e].wait(eng, u - 1)
                    for k in range(TPB):
                        i = eng.transpose(tb[:, k * P:(k + 1) * P], PR[j % 2][:, k * P:(k + 1) * P], ident[:, :])
                    pt.inc(i)
                if name == pe[e].owner:
                    pt.wait(eng, u, j)
                    av.wait(eng, u - 2)
                    dst = PTS[par][e][:, :, qt * P:(qt + 1) * P]
                    src = tb[:, :].rearrange("p (k q) -> p k q", k=TPB)
                    pe[e].inc(eng.tensor_copy(dst, src) if e == 0 else eng.activation(dst, src, ACT.Copy))

            def times_v(name, eng, u, par, k):
                if name == "pe":
                    if k == 0:
                        pja.wait(eng, u, 2)
                        for e in range(2):
                            pe[e].wait(eng, u)
                        ov.wait(eng, u - 1)
                    for e in range(2):
                        i = eng.matmul(bank[6][e * DH:(e + 1) * DH, :], V[par][:, k, e * DH:(e + 1) * DH],
                                       PTS[par][e][:, k, :], start=(k == 0), stop=(k == TPB - 1))
                    if k == TPB - 1:
                        av.inc(i)
                if name == "act" and k == TPB - 1:
                    av.wait(eng, u)
                    yy.wait(eng, u - 1)
                    ov.inc(eng.activation(OT[:, :], bank[6][:, :], ACT.Copy))

            def project_out(name, eng, u, par):
                if name == "pe":
                    ov.wait(eng, u)
                    xa.wait(eng, u - 1)
                    for t in range(TPB):
                        i = eng.matmul(bank[7][:, t * P:(t + 1) * P], OT[:, t * P:(t + 1) * P],
                                       WR[:, u % PAIRS, :], start=True, stop=True)
                    yy.inc(i)
                if name == "dve":
                    yy.wait(eng, u)
                    xa.wait(eng, u - 1)
                    xs = X[:, bass.ds((u // PAIRS) * TPB, TPB), :]
                    xa.inc(eng.tensor_tensor(xs, xs, bank[7][:, :].rearrange("p (t e) -> p t e", t=TPB), ALU.add))

            def head(name, eng, u, par, j):
                scores(name, eng, u, par, j)
                softmax(name, eng, u, par, j)

            def pair(name, eng, u, par, prev=True, nxt=True):
                if nxt:
                    stage(name, eng, u + 1, 1 - par)
                for j in range(NJ):
                    ahead = (u, par, j + 2) if j + 2 < NJ else (u + 1, 1 - par, j + 2 - NJ)
                    if nxt or j + 2 < NJ:
                        head(name, eng, *ahead)
                    transpose_p(name, eng, u, par, j)
                    if nxt or j + 2 < NJ:
                        normalise(name, eng, *ahead)
                    if prev and j < TPB:
                        times_v(name, eng, u - 1, 1 - par, j)
                    if nxt and j in (3, 4, 5):
                        project(name, eng, u + 1, 1 - par, j - 3)
                    if prev and j == 6:
                        project_out(name, eng, u - 1, 1 - par)

            def attn_program(name, eng):
                if name == "sp":
                    return
                stage(name, eng, 0, 0)
                for c in range(3):
                    project(name, eng, 0, 0, c)
                for j in range(2):
                    head(name, eng, 0, 0, j)
                    normalise(name, eng, 0, 0, j)
                if name == "pool":
                    clear_and_mask(eng)
                last = BATCH * PAIRS - 1
                pair(name, eng, 0, 0, prev=False)
                with eng.Fori(0, last // 2) as v:
                    for i in (1, 2):
                        pair(name, eng, 2 * v + i, i % 2)
                pair(name, eng, last, last % 2, nxt=False)
                for k in range(TPB):
                    times_v(name, eng, last, last % 2, k)
                project_out(name, eng, last, last % 2)

            engines_run(nc, sigs0, attn_program)

        with ExitStack() as ctx:
            def sbl(name, shape, dt=F32):
                return sb(name, shape, dt, ctx)

            WQKV = sbl("WQKV", [P, 2, 3 * INNER])
            WO = sbl("WO", [P, 2, PAIRS, E])
            W1 = sbl("W1", [P, 2, 2 * FF])
            W2 = sbl("W2", [P, 2, len(FFC), E])
            QKS = sbl("QKS", [P, 2, 2, DH])
            B1 = sbl("B1", [P, 2, 2 * FF])
            B2 = sbl("B2", [P, 2, E])
            ROT = sbl("ROT", [P, 4, TPB, DH])
            RT = sbl("RT", [P, 4, TPB, DH])

            XS = [sbl(f"XS{i}", [P, E]) for i in range(2)]
            QR = sbl("QR", [P, 4, 512])
            SQ = [sbl(f"SQ{i}", [P, 512]) for i in range(2)]
            T2 = [sbl(f"T2{i}", [P, 512]) for i in range(2)]
            TQ = sbl("TQ", [P, 4, 512])
            SS = sbl("SS", [P, 4, 8])
            SM = sbl("SM", [P, 4, 8])
            RN = sbl("RN", [P, 4, 8])
            VG = [sbl(f"VG{i}", [SPAN, 2, INNER]) for i in range(2)]
            QTL = sbl("QTL", [P, 2, PAIRS, P])
            PL = [sbl(f"PL{i}", [P, HG, SPAN]) for i in range(2)]
            NML = sbl("NML", [P, HEADS])
            RSL = sbl("RSL", [P, HEADS])
            RIL = sbl("RIL", [P, HEADS])
            PTL = [sbl(f"PTL{i}", [SPAN, HG * P]) for i in range(2)]
            OTL = sbl("OTL", [P, PAIRS, P])
            X2 = sbl("X2", [P, TPB, E])
            X2B = sbl("X2B", [P, 2, TPB, E])
            XNT2 = sbl("XNT2", [P, SEQ])
            A1 = sbl("A1", [P, TPB, FF])
            G1 = sbl("G1", [P, TPB, FF])
            HT = [sbl(f"HT{i}", [P, len(FFC), P]) for i in range(2)]

            s_i = ctx.enter_context(nc.semaphore("s_i"))
            s_m = ctx.enter_context(nc.semaphore("s_m"))
            s_w = ctx.enter_context(nc.semaphore("s_w"))
            NW = 10

            def sig(name, per, owner, lag=1):
                s = Sig(nc, ctx, "l_" + name, per, owner, lag)
                sigs.append(s)
                return s
            sigs = []
            xs = sig("xs", 1, "act")
            fx = sig("fx", 1, "pe")
            fxd = sig("fxd", 1, "dve")
            fxa = sig("fxa", 1, "act")
            ch = sig("ch", 6, "pe")
            cv = sig("cv", 6, "act")
            sq = sig("sq", 4, "act")
            ss = sig("ss", 4, "dve")
            sm = sig("sm", 2, "dve")
            rn = sig("rn", 2, "pool")
            t1 = sig("t1", 4, "dve")
            t2 = sig("t2", 4, "pool")
            ad = sig("ad", 4, "dve")
            qn = sig("qn", 2, "pool")
            kn = sig("kn", 2, "dve")
            tr = sig("tr", 4, "pe")
            qe = sig("qe", 2, "act")
            ke0 = sig("ke0", 2, "dve")
            ke1 = sig("ke1", 2, "act")
            scl = sig("scl", NHG, "pe", 2)
            nml = sig("nml", NHG, "dve")
            exl = sig("exl", NHG, "act")
            ril = sig("ril", NHG, "dve")
            pnl = sig("pnl", NHG, "dve")
            ptl = sig("ptl", NHG, "pe")
            pcl = sig("pcl", NHG, "act")
            avl = sig("avl", NHG, "pe", 2)
            ovl = sig("ovl", 2, "act")
            yl = sig("yl", 1, "pe")
            x2 = sig("x2", 1, "dve", 2)
            x2b = sig("x2b", 1, "pool", TPB)
            rtd = sig("rtd", 2, "dve")
            rtp = sig("rtp", 4, "pool")
            g1 = sig("g1", 1, "pe")
            g1d = sig("g1d", 1, "dve")
            g1a = sig("g1a", 1, "act")
            g2 = sig("g2", 1, "pe")
            gst = sig("gst", 5, "dve")
            gve = sig("gve", 1, "dve")
            grs = sig("grs", 1, "pool")
            gxn = sig("gxn", 1, "dve")
            g3 = sig("g3", 1, "pe")
            gxt = sig("gxt", 1, "act")
            hh = sig("hh", 2 * TPB, "pe")
            hb = sig("hb", 2 * TPB, "dve")
            ge = sig("ge", 1, "act")
            hm = sig("hm", TPB, "pool")
            ht = sig("ht", TPB, "pe")
            he = sig("he", TPB, "act")
            fy = sig("fy", TPB, "pe")
            fin = sig("fin", TPB, "dve", 3)

            def load_layer(eng, l, par, sem):
                at = l if isinstance(l, slice) or not isinstance(l, int) else slice(l, l + 1)

                def one(w):
                    return w[at].rearrange("l r c -> (l r) c")

                def d(dst, src):
                    eng.dma_start(dst, src).then_inc(sem, 16)
                half = 3 * INNER // 2
                for i in range(2):
                    d(WQKV[:, par, i * half:(i + 1) * half], one(wqkv)[:, i * half:(i + 1) * half])
                d(WO[:, par, :, :], one(wo).rearrange("(c p) e -> p c e", p=P))
                d(W1[:, par, :], one(w1))
                c0, n = FFC[-1]
                d(W2[:, par, 0:2, :], one(w2)[0:c0, :].rearrange("(c p) e -> p c e", p=P))
                d(W2[0:n, par, len(FFC) - 1, :], one(w2)[c0:c0 + n, :])
                d(QKS[:, par, 0, :], qscale[at, :].to_broadcast([P, DH]))
                d(QKS[:, par, 1, :], kscale[at, :].to_broadcast([P, DH]))
                d(B1[:, par, :], b1[at, :].to_broadcast([P, 2 * FF]))
                d(B2[:, par, :], b2[at, :].to_broadcast([P, E]))

            def ln_gains(name, eng):
                n = 2 * DEPTH
                if name == "pe":
                    eng.wait_ge(s_i, 48)
                    eng.transpose(bank[5][:, 0:n], LGB[:, :], ident[0:n, 0:n]).then_inc(s_g, 1)
                if name == "dve":
                    eng.wait_ge(s_g, 1)
                    eng.tensor_copy(GBA[:, :, :], bank[5][:, 0:n].rearrange("p (k l) -> p k l", k=2))\
                       .then_inc(s_g, 1)
                if name in ("pe", "act"):
                    eng.wait_ge(s_g, 2)

            LGB = sbl("LGB", [2 * DEPTH, E])
            GBA = sbl("GBA", [P, 2, DEPTH])
            s_g = ctx.enter_context(nc.semaphore("s_g"))

            def rotary_tables(name, eng, s, first=False):
                lp = (s // BATCH) % 2
                if name == "dve":
                    if first:
                        eng.wait_ge(s_i, 48)
                    wait_weights(eng, s)
                    t1.wait(eng, s * TPB - 1)
                    for k in range(2):
                        q = QKS[:, lp, k:k + 1, :].to_broadcast([P, TPB, DH])
                        rtd.inc(eng.tensor_tensor(RT[:, 2 * k, :, :], ROT[:, 2 * k, :, :], q, ALU.mult))
                if name == "pool":
                    if first:
                        eng.wait_ge(s_i, 48)
                    wait_weights(eng, s)
                    t2.wait(eng, s * TPB - 1)
                    settle(eng)
                    for k in range(2):
                        for h in range(2):
                            q = QKS[:, lp, k:k + 1, (1 - h) * 32:(2 - h) * 32].to_broadcast([P, TPB, 32])
                            a = slice(h * 32, h * 32 + 32)
                            rtp.inc(eng.tensor_tensor(RT[:, 2 * k + 1, :, a], ROT[:, 2 * k + 1, :, a], q, ALU.mult))

            def wait_weights(eng, s):
                eng.wait_ge(s_w, (s // BATCH + 1) * 16 * NW)

            def stage_x(name, eng, s, t):
                g = s * TPB + t
                b = s % BATCH
                if name == "act":
                    fx.wait(eng, g - 1)
                    fin.wait(eng, s - 3)
                    xs.inc(eng.activation(XS[t % 2][:, :], X[:, b * TPB + t, :], ACT.Copy))

            def front_x(name, eng, s, t):
                g = s * TPB + t
                if name == "pe":
                    xs.wait(eng, g)
                    x2.wait(eng, g - 2)
                    fx.inc(eng.transpose(bank[7][:, 0:P], XS[t % 2][:, :], ident[:, :]))
                c0 = t * P
                if name == "dve":
                    fx.wait(eng, g)
                    fxd.inc(eng.tensor_copy(XT[0:DH, c0:c0 + P], bank[7][0:DH, 0:P]))
                if name == "act":
                    fx.wait(eng, g)
                    fxa.inc(eng.activation(XT[DH:P, c0 + 1:c0 + 1 + P], bank[7][DH:P, 0:P], ACT.Copy))

            s_v = [ctx.enter_context(nc.semaphore(f"s_v{i}")) for i in range(2)]

            def v_placed(eng, s, t):
                eng.wait_ge(s_v[t % 2], (2 * s + t // 2 + 2) * 48)

            def place_v(name, eng, s, t):
                g = s * TPB + t
                if name == "sp":
                    cv.wait(eng, g)
                    avl.wait(eng, g - 2)
                    v, o = VN[t % 2], VG[t % 2]
                    before = VN[1 - t % 2][P - WIN:P, :] if t else none[:, :]
                    for dst, src in ((o[0:WIN, 0, :], before), (o[WIN:SPAN, 0, :], v[0:GRP, :]),
                                     (o[:, 1, :], v[WIN:P, :])):
                        eng.dma_start(dst, src).then_inc(s_v[t % 2], 16)

            def front_chunk(name, eng, s, t, c):
                g = s * TPB + t
                lp = (s // BATCH) % 2
                pb = bank[c % 2]
                if name == "pe":
                    if c == 0:
                        fxd.wait(eng, g)
                        fxa.wait(eng, g)
                        wait_weights(eng, s)
                    if c >= 2:
                        cv.wait(eng, g, c - 2)
                    else:
                        cv.wait(eng, g - 1, 4 + c)
                    ch.inc(eng.matmul(pb[:, :], XT[:, t * P:(t + 1) * P], WQKV[:, lp, c * 512:(c + 1) * 512],
                                      start=True, stop=True))
                if name == "act":
                    ch.wait(eng, g, c)
                    if c < 4:
                        t1.wait(eng, g - 1, c)
                        t2.wait(eng, g - 1, c)
                        cv.inc(eng.activation(QR[:, c, :], pb[:, :], ACT.Copy))
                    else:
                        if t:
                            v_placed(eng, s, t - 1)
                        else:
                            v_placed(eng, s - 1, TPB - 1)
                        cv.inc(eng.activation(VN[t % 2][:, (c - 4) * 512:(c - 3) * 512], pb[:, :], ACT.Copy))

            def front_products(name, eng, s, t, c):
                g = s * TPB + t
                k = c // 2
                q3 = QR[:, c, :].rearrange("p (h d) -> p h d", d=DH)
                if name == "dve":
                    cv.wait(eng, g, c)
                    tr.wait(eng, g - 1, c)
                    if c == 0:
                        rtd.wait(eng, s)
                    cos = RT[:, 2 * k, t:t + 1, :].to_broadcast([P, 8, DH])
                    tq = TQ[:, c, :].rearrange("p (h d) -> p h d", d=DH)
                    t1.inc(eng.tensor_tensor(tq, q3, cos, ALU.mult))
                if name == "pool":
                    cv.wait(eng, g, c)
                    if c >= 2:
                        ad.wait(eng, g, c - 2)
                    else:
                        ad.wait(eng, g - 1, 2 + c)
                    if c == 0:
                        rtp.wait(eng, s)
                    settle(eng)
                    o3 = T2[c % 2][:, :].rearrange("p (h d) -> p h d", d=DH)
                    for h in range(2):
                        sin = RT[:, 2 * k + 1, t:t + 1, h * 32:h * 32 + 32].to_broadcast([P, 8, 32])
                        i = eng.tensor_tensor(o3[:, :, h * 32:h * 32 + 32],
                                              q3[:, :, (1 - h) * 32:(2 - h) * 32], sin, ALU.mult)
                    t2.inc(i)

            def front_squares(name, eng, s, t, c):
                g = s * TPB + t
                k = c // 2
                if name == "dve":
                    sq.wait(eng, g, c)
                    sm.wait(eng, g - 1, k)
                    ss.inc(eng.tensor_reduce(SS[:, c, :], SQ[c % 2][:, :].rearrange("p (h d) -> p h d", d=DH),
                                             AX.X, ALU.add))
                if name == "act":
                    cv.wait(eng, g, c)
                    if c >= 2:
                        ss.wait(eng, g, c - 2)
                    else:
                        ss.wait(eng, g - 1, 2 + c)
                    sq.inc(eng.activation(SQ[c % 2][:, :], QR[:, c, :], ACT.Square))

            def front_norms(name, eng, s, t, k):
                g = s * TPB + t
                if name == "dve":
                    ss.wait(eng, g, 2 * k + 1)
                    rn.wait(eng, g - 1, k)
                    sm.inc(eng.tensor_scalar(SM[:, 2 * k:2 * k + 2, :], SS[:, 2 * k:2 * k + 2, :], NORM2_EPS,
                                             None, ALU.max))
                if name == "pool":
                    sm.wait(eng, g, k)
                    (kn if k else qn).wait(eng, g - 1)
                    rn.inc(eng.tensor_tensor(RN[:, 2 * k:2 * k + 2, :], SM[:, 2 * k:2 * k + 2, :],
                                             mhalf[:, 0:16].rearrange("p (c h) -> p c h", c=2), ALU.pow))

            def front_sum(name, eng, s, t, c):
                g = s * TPB + t
                if name == "dve":
                    t2.wait(eng, g, c)
                    t1.wait(eng, g, c)
                    ad.inc(eng.tensor_tensor(TQ[:, c, :], TQ[:, c, :], T2[c % 2][:, :], ALU.add))

            def front_scale(name, eng, s, t, c):
                g = s * TPB + t
                k = c // 2
                if name == ("dve" if k else "pool"):
                    rn.wait(eng, g, k)
                    ad.wait(eng, g, c)
                    tq = TQ[:, c, :].rearrange("p (h d) -> p h d", d=DH)
                    r = RN[:, c, :].rearrange("p (h a) -> p h a", a=1).to_broadcast([P, 8, DH])
                    (kn if k else qn).inc(eng.tensor_tensor(tq, tq, r, ALU.mult))

            def feature_major(name, eng, s, t, c):
                g = s * TPB + t
                tb = bank[5]
                if name == "pe":
                    (kn if c >= 2 else qn).wait(eng, g, c % 2)
                    if c == 0:
                        ke0.wait(eng, g - 1)
                        ke1.wait(eng, g - 1)
                        if t == 2:
                            hb.wait(eng, s - 1, 2 * UP_FIRST - 1)
                        if t == 3:
                            hb.wait(eng, s - 1)
                    elif c < 3:
                        qe.wait(eng, g, c - 1)
                    else:
                        ke0.wait(eng, g, 0)
                        ke1.wait(eng, g, 0)
                    for i in range(4):
                        m = eng.transpose(tb[:, i * P:(i + 1) * P], TQ[:, c, i * P:(i + 1) * P], ident[:, :])
                    tr.inc(m)
                v4 = tb[:, :].rearrange("p (i q) -> p i q", i=4)
                if name == "act":
                    tr.wait(eng, g, c)
                    if c < 2:
                        scl.wait(eng, g - 2)
                        qe.inc(eng.activation(QTL[:, t % 2, 4 * c:4 * c + 4, :], v4, ACT.Copy))
                    else:
                        if t == 0:
                            scl.wait(eng, g - 1)
                        a = 4 * (c - 2)
                        ke1.inc(eng.activation(KZL[DH:P, a:a + 4, 1, WIN + t * P:WIN + (t + 1) * P],
                                               v4[DH:P, :, :], ACT.Copy))
                if name == "dve" and c >= 2:
                    tr.wait(eng, g, c)
                    if t == 0:
                        scl.wait(eng, g - 1)
                    a = 4 * (c - 2)
                    ke0.inc(eng.tensor_copy(KZL[0:DH, a:a + 4, 0, WIN + t * P:WIN + (t + 1) * P], v4[0:DH, :, :]))

            def local_scores(name, eng, s, t, hg):
                g = s * TPB + t
                sbk = bank[2 + hg % 2]
                n = HG * SPAN
                if name == "pe":
                    if hg % 2 == 0:
                        qe.wait(eng, g, hg // 2)
                        ke0.wait(eng, g, hg // 2)
                        ke1.wait(eng, g, hg // 2)
                    if hg >= 2:
                        exl.wait(eng, g, hg - 2)
                    else:
                        exl.wait(eng, g - 1, 2 + hg)
                    eng.matmul(sbk[:, 0:n], identb[:, :], band[:, 0 if t == 0 else 1, :, :]
                               .rearrange("p h j -> p (h j)"), start=True, stop=False, skip_group_check=True)
                    for pl in range(2):
                        pr = 2 * hg + pl
                        for grp in range(2):
                            k0 = t * P + grp * GRP
                            m = eng.matmul(sbk[grp * GRP:(grp + 1) * GRP, pl * 2 * SPAN:(pl + 1) * 2 * SPAN],
                                           QTL[:, t % 2, pr, grp * GRP:(grp + 1) * GRP], KZL[:, pr, :, k0:k0 + SPAN],
                                           start=False, stop=(pl == 1), skip_group_check=True)
                    scl.inc(m)

            def local_max(name, eng, s, t, hg):
                g = s * TPB + t
                cols = slice(HG * hg, HG * hg + HG)
                if name == "dve":
                    scl.wait(eng, g, hg)
                    exl.wait(eng, g - 1, hg)
                    s3 = bank[2 + hg % 2][:, 0:HG * SPAN].rearrange("p (h j) -> p h j", h=HG)
                    nml.inc(eng.tensor_reduce(NML[:, cols], s3, AX.X, ALU.max, negate=True))

            def local_softmax(name, eng, s, t, hg):
                g = s * TPB + t
                s3 = bank[2 + hg % 2][:, 0:HG * SPAN].rearrange("p (h j) -> p h j", h=HG)
                pl = PL[hg % 2]
                cols = slice(HG * hg, HG * hg + HG)
                if name == "act":
                    nml.wait(eng, g, hg)
                    ril.wait(eng, g - 1, hg)
                    if hg >= 2:
                        ptl.wait(eng, g, hg - 2)
                    else:
                        ptl.wait(eng, g - 1, 2 + hg)
                    for h in range(HG):
                        c = HG * hg + h
                        i = eng.activation(pl[:, h, :], s3[:, h, :], ACT.Exp, bias=NML[:, c:c + 1],
                                           accum_out=RSL[:, c:c + 1])
                    exl.inc(i)

            def local_reciprocal(name, eng, s, t, hg):
                g = s * TPB + t
                cols = slice(HG * hg, HG * hg + HG)
                if name == "dve":
                    exl.wait(eng, g, hg)
                    pnl.wait(eng, g - 1, hg)
                    ril.inc(eng.reciprocal(RIL[:, cols], RSL[:, cols]))

            def local_normalise(name, eng, s, t, hg):
                g = s * TPB + t
                cols = slice(HG * hg, HG * hg + HG)
                if name == "dve":
                    ril.wait(eng, g, hg)
                    pl = PL[hg % 2]
                    r = RIL[:, cols].rearrange("p (h a) -> p h a", a=1).to_broadcast([P, HG, SPAN])
                    pnl.inc(eng.tensor_tensor(pl[:, :, :], pl[:, :, :], r, ALU.mult))

            def local_transpose(name, eng, s, t, hg):
                g = s * TPB + t
                if name == "pe":
                    pnl.wait(eng, g, hg)
                    if hg:
                        pcl.wait(eng, g, hg - 1)
                    else:
                        pcl.wait(eng, g - 1)
                    for h in range(HG):
                        i = eng.transpose(bank[4][0:SPAN, h * P:(h + 1) * P], PL[hg % 2][:, h, :], ident[:, :])
                    ptl.inc(i)
                if name == "act":
                    ptl.wait(eng, g, hg)
                    if hg >= 2:
                        avl.wait(eng, g, hg - 2)
                    else:
                        avl.wait(eng, g - 1, 2 + hg)
                    pcl.inc(eng.activation(PTL[hg % 2][:, :], bank[4][0:SPAN, :], ACT.Copy))

            def local_av(name, eng, s, t, hg):
                g = s * TPB + t
                if name == "pe":
                    pcl.wait(eng, g, hg)
                    if hg == 0:
                        v_placed(eng, s, t)
                        ovl.wait(eng, g - 1)
                    if hg == 2:
                        ovl.wait(eng, g, 0)
                    for h in range(HG):
                        head = HG * hg + h
                        pl, e = divmod(head % 8, 2)
                        for grp in range(2):
                            o0 = pl * P + grp * GRP
                            i = eng.matmul(bank[6][e * DH:(e + 1) * DH, o0:o0 + GRP],
                                           VG[t % 2][:, grp, head * DH:(head + 1) * DH],
                                           PTL[hg % 2][:, h * P + grp * GRP:h * P + (grp + 1) * GRP],
                                           start=True, stop=True)
                    avl.inc(i)
                if name == "act" and hg % 2:
                    avl.wait(eng, g, hg)
                    yl.wait(eng, g - 1)
                    ovl.inc(eng.activation(OTL[:, 2 * hg - 2:2 * hg + 2, :],
                                           bank[6][:, :].rearrange("p (i q) -> p i q", i=4), ACT.Copy))

            def local_out(name, eng, s, t, half):
                g = s * TPB + t
                lp = (s // BATCH) % 2
                if name == "pe":
                    ovl.wait(eng, g, half)
                    if half == 0:
                        if t == 0:
                            gxt.wait(eng, s - 1)
                        elif t == 1:
                            hb.wait(eng, s - 1, 2 * UP_FIRST - 1)
                        elif t == 2:
                            hb.wait(eng, s - 1)
                        else:
                            fin.wait(eng, s - 1)
                        if isinstance(g, int) and g == STEPS * TPB - 1:
                            x2.wait(eng, g - 1)
                        else:
                            fxd.wait(eng, g + 1)
                            fxa.wait(eng, g + 1)
                    for pr in range(4 * half, 4 * half + 4):
                        i = eng.matmul(bank[7][:, 0:E], OTL[:, pr, :], WO[:, lp, pr, :],
                                       start=(pr == 0), stop=(pr == PAIRS - 1))
                    if half:
                        yl.inc(i)
                if name == "dve" and half:
                    yl.wait(eng, g)
                    g1.wait(eng, s - 1)
                    x2b.wait(eng, g - TPB)
                    x2.inc(eng.tensor_tensor(X2[:, t, :], bank[7][:, 0:E], X[:, (s % BATCH) * TPB + t, :], ALU.add))

            def residual(name, eng, s, t):
                g = s * TPB + t
                lp = (s // BATCH) % 2
                if name == "pool":
                    x2.wait(eng, g)
                    fin.wait(eng, s - 2)
                    settle(eng)
                    x2b.inc(eng.tensor_tensor(X2B[:, s % 2, t, :], X2[:, t, :], B2[:, lp, :], ALU.add))

            m = bank[7]
            m3 = m[:, :].rearrange("p (t e) -> p t e", t=TPB)

            def ffn_turn(name, eng, s, alone=False):
                if name == "pe":
                    x2.wait(eng, s * TPB + TPB - 1)
                    if not alone:
                        fxd.wait(eng, (s + 1) * TPB + 1)
                        fxa.wait(eng, (s + 1) * TPB + 1)
                    for t in range(TPB):
                        i = eng.transpose(m[:, t * P:(t + 1) * P], X2[:, t, :], ident[:, :])
                    g1.inc(i)
                if name == "dve":
                    g1.wait(eng, s)
                    g3.wait(eng, s - 1)
                    g1d.inc(eng.tensor_copy(XT2[0:DH, 0:SEQ], m[0:DH, :]))
                if name == "act":
                    g1.wait(eng, s)
                    g3.wait(eng, s - 1)
                    g1a.inc(eng.activation(XT2[DH:P, 1:SEQ + 1], m[DH:P, :], ACT.Copy))

            def ffn_norm(name, eng, s):
                if name == "pe":
                    g1d.wait(eng, s)
                    g1a.wait(eng, s)
                    for t in range(TPB):
                        i = eng.transpose(m[:, t * P:(t + 1) * P], XT2[:, t * P:(t + 1) * P], ident[:, :])
                    g2.inc(i)
                if name == "dve":
                    g2.wait(eng, s)
                    for t in range(TPB):
                        gst.inc(eng.bn_stats(stats[:, t, :], m3[:, t, :]))
                    gst.wait(eng, s, TPB - 1)
                    settle(eng)
                    for t in range(TPB):
                        i = eng.bn_aggr(mv[:, t, :], stats[:, t, :])
                    gst.inc(i)
                    gst.wait(eng, s)
                    gve.inc(eng.tensor_scalar(veps[:, :], mv[:, :, 1], LN_EPS, None, ALU.add))
                if name == "pool":
                    gve.wait(eng, s)
                    gxn.wait(eng, s - 1)
                    grs.inc(eng.tensor_tensor(rstd[:, :], veps[:, :], mhalf[:, 0:TPB], ALU.pow))

            def ffn_norm2(name, eng, s):
                if name == "dve":
                    grs.wait(eng, s)
                    for t in range(TPB):
                        i = eng.tensor_scalar(XT2[:, 1 + t * P:1 + (t + 1) * P], m3[:, t, :], mv[:, t, 0:1],
                                              rstd[:, t:t + 1], ALU.subtract, ALU.mult)
                    gxn.inc(i)

            def ffn_gain(name, eng, s):
                if name == "pe":
                    gxn.wait(eng, s)
                    for t in range(TPB):
                        i = eng.transpose(m[:, t * P:(t + 1) * P], XT2[:, 1 + t * P:1 + (t + 1) * P], ident[:, :])
                    g3.inc(i)
                if name == "act":
                    g3.wait(eng, s)
                    hh.wait(eng, s - 1)
                    gsel = GBA[:, 0, bass.ds(s // BATCH, 1)]
                    bsel = GBA[:, 1, bass.ds(s // BATCH, 1)]
                    gxt.inc(eng.activation(XNT2[:, :], m[:, :], ACT.Identity, scale=gsel, bias=bsel))

            def ffn_up(name, eng, s, t):
                lp = (s // BATCH) % 2
                up = (bank[5], bank[7])
                dst = (A1, G1)
                if name == "pe":
                    gxt.wait(eng, s)
                    if t == 0:
                        later = not isinstance(s, int) or s < STEPS - 1
                        ke0.wait(eng, (s + 1) * TPB + 1 if later else s * TPB + TPB - 1)
                        ke1.wait(eng, (s + 1) * TPB + 1 if later else s * TPB + TPB - 1)
                        if later:
                            fxd.wait(eng, (s + 1) * TPB + 2)
                            fxa.wait(eng, (s + 1) * TPB + 2)
                    if t == UP_FIRST and (not isinstance(s, int) or s < STEPS - 1):
                        for x in (ke0, ke1):
                            x.wait(eng, (s + 1) * TPB + 2)
                        for x in (fxd, fxa):
                            x.wait(eng, (s + 1) * TPB + 3)
                    for k in range(2):
                        if t:
                            hb.wait(eng, s, 2 * (t - 1) + k)
                        hh.inc(eng.matmul(up[k][:, 0:FF], XNT2[:, t * P:(t + 1) * P],
                                          W1[:, lp, k * FF:(k + 1) * FF], start=True, stop=True))
                if name == "dve":
                    for k in range(2):
                        hh.wait(eng, s, 2 * t + k)
                        if k == 0:
                            ht.wait(eng, s - 1)
                        else:
                            hm.wait(eng, s - 1)
                        hb.inc(eng.tensor_tensor(dst[k][:, t, :], up[k][:, 0:FF],
                                                 B1[:, lp, k * FF:(k + 1) * FF], ALU.add))

            def ffn_gelu(name, eng, s):
                if name == "act":
                    hb.wait(eng, s)
                    ge.inc(eng.activation(G1[:, :, :], G1[:, :, :], ACT.Gelu))
                if name == "pool":
                    ge.wait(eng, s)
                    for t in range(TPB):
                        hm.inc(eng.tensor_tensor(A1[:, t, :], A1[:, t, :], G1[:, t, :], ALU.mult))

            def ffn_turn_h(name, eng, s, t):
                tb = bank[5]
                if name == "pe":
                    hm.wait(eng, s, t)
                    if t:
                        he.wait(eng, s, t - 1)
                    else:
                        later = not isinstance(s, int) or s < STEPS - 1
                        if later:
                            ke0.wait(eng, (s + 1) * TPB + 3)
                            ke1.wait(eng, (s + 1) * TPB + 3)
                        hb.wait(eng, s)
                    for c, (c0, n) in enumerate(FFC):
                        i = eng.transpose(tb[0:n, c * P:(c + 1) * P], A1[:, t, c0:c0 + n], ident[:, :])
                    ht.inc(i)
                if name == "act":
                    ht.wait(eng, s, t)
                    if t >= 2:
                        fy.wait(eng, s, t - 2)
                    else:
                        fy.wait(eng, s - 1, 2 + t)
                    nf = len(FFC) - 1
                    n = FFC[nf][1]
                    eng.activation(HT[t % 2][:, 0:nf, :], tb[:, 0:nf * P].rearrange("p (c q) -> p c q", c=nf),
                                   ACT.Copy)
                    he.inc(eng.activation(HT[t % 2][0:n, nf, :], tb[0:n, nf * P:(nf + 1) * P], ACT.Copy))

            def ffn_down(name, eng, s, t):
                lp = (s // BATCH) % 2
                if name == "pe":
                    he.wait(eng, s, t)
                    if t:
                        fin.wait(eng, s, t - 1)
                    else:
                        if not isinstance(s, int) or s < STEPS - 2:
                            fxd.wait(eng, (s + 2) * TPB)
                            fxa.wait(eng, (s + 2) * TPB)
                        elif s == STEPS - 2:
                            x2.wait(eng, (s + 1) * TPB + 2)
                    for c, (c0, n) in enumerate(FFC):
                        i = eng.matmul(m[:, 0:E], HT[t % 2][0:n, c, :], W2[0:n, lp, c, :],
                                       start=(c == 0), stop=(c == len(FFC) - 1))
                    fy.inc(i)
                if name == "dve":
                    fy.wait(eng, s, t)
                    x2b.wait(eng, s * TPB + t)
                    fin.inc(eng.tensor_tensor(X[:, (s % BATCH) * TPB + t, :], m[:, 0:E],
                                              X2B[:, s % 2, t, :], ALU.add))

            def ffn_alone(name, eng, s):
                ffn_turn(name, eng, s, alone=True)
                ffn_norm(name, eng, s)
                ffn_norm2(name, eng, s)
                ffn_gain(name, eng, s)
                for t in range(TPB):
                    ffn_up(name, eng, s, t)
                ffn_gelu(name, eng, s)
                for t in range(TPB):
                    ffn_turn_h(name, eng, s, t)
                    ffn_down(name, eng, s, t)

            def own(f, *arg):
                return lambda name, eng, s, t, last: f(name, eng, s, t, *arg)

            def following(f, *arg):
                def run(name, eng, s, t, last):
                    if not last:
                        fs, ft = (s, t + 1) if t < TPB - 1 else (s + 1, 0)
                        f(name, eng, fs, ft, *arg)
                return run

            def tables(name, eng, s, t, last):
                if t == TPB - 1 and not last:
                    rotary_tables(name, eng, s + 1)

            def batch_before(f, *arg):
                return lambda name, eng, s, t, last: f(name, eng, s - 1, *arg)

            actions = {"tables": tables, "stage_x": following(stage_x), "x": following(front_x), "out0": own(local_out, 0), "out1": own(local_out, 1), "resid": own(residual),
                       "turn": batch_before(ffn_turn), "stat": batch_before(ffn_norm),
                       "norm": batch_before(ffn_norm2), "gain": batch_before(ffn_gain),
                       "gelu": batch_before(ffn_gelu)}
            for c in range(4):
                actions.update({f"turn_qk{c}": own(feature_major, c), f"score{c}": own(local_scores, c),
                                f"exp{c}": own(local_softmax, c), f"div{c}": own(local_normalise, c),
                                f"turn_p{c}": own(local_transpose, c), f"av{c}": own(local_av, c),
                                f"rot{c}": following(front_products, c), f"sq{c}": following(front_squares, c),
                                f"sum{c}": following(front_sum, c),
                                f"max{c}": own(local_max, c), 
                                f"scale{c}": following(front_scale, c),
                                f"recip{c}": own(local_reciprocal, c),
                                f"up{c}": batch_before(ffn_up, c), f"turn_h{c}": batch_before(ffn_turn_h, c),
                                f"down{c}": batch_before(ffn_down, c)})
            for c in range(6):
                actions[f"chunk{c}"] = following(front_chunk, c)
            for k in range(2):
                actions[f"pow{k}"] = following(front_norms, k)

            def slot(name, eng, s, t, last=False, with_ffn=True, first=False, after=False):
                for entry in ORDER[name].split():
                    at, key = entry.split(":") if ":" in entry else (None, entry)
                    if key.startswith("~"):
                        if not first:
                            ps, pt = (s, t - 1) if t else (s - 1, TPB - 1)
                            actions[key[1:]](name, eng, ps, pt, after)
                    elif not after and (at is None or (with_ffn and int(at) == t)):
                        actions[key](name, eng, s, t, last)

            def layers_program(name, eng):
                if name == "sp":
                    in_dma(eng, s_i, ROT[:, :, :, :], rot.rearrange("k (t p) d -> p k t d", p=P))
                    in_dma(eng, s_i, LGB[0:DEPTH, :], lng)
                    in_dma(eng, s_i, LGB[DEPTH:2 * DEPTH, :], lnb)
                    for i in range(2):
                        eng.sem_inc(s_v[i], 48)
                    load_layer(eng, 0, 0, s_w)
                    eng.wait_ge(s_k, 11)

                    def steps_v(first, n):
                        with eng.Fori(0, n) as i:
                            for t in range(TPB):
                                place_v(name, eng, first + i, t)

                    with eng.Fori(0, DEPTH - 1) as l:
                        for t in range(TPB + 1):
                            place_v(name, eng, l * BATCH + t // TPB, t % TPB)
                        fin.wait(eng, l * BATCH - 1)
                        rtd.wait(eng, l * BATCH)
                        eng.wait_ge(s_w, (l + 1) * 16 * NW)
                        load_layer(eng, bass.ds(l + 1, 1), (l + 1) % 2, s_w)
                        for t in range(1, TPB):
                            place_v(name, eng, l * BATCH + 1, t)
                        steps_v(l * BATCH + 2, BATCH - 2)
                    steps_v((DEPTH - 1) * BATCH, BATCH)
                    eng.wait_ge(s_w, DEPTH * 16 * NW)
                    eng.wait_ge(s_i, 48)
                    for t in (TPB - 2, TPB - 1):
                        v_placed(eng, STEPS - 1, t)
                    return
                if name == "dve":
                    i = eng.tensor_copy(XM[:, :, :], X[:, :, :])
                    i.then_inc(s_m, 1)
                    eng.wait_ge(s_m, 1)
                if name in ("dve", "pool"):
                    with eng.Fori(0, BATCH) as b:
                        ln2(name, eng, b)
                if name == "pool":
                    lx.wait(eng, BATCH - 1)
                if name != "sp":
                    eng.wait_ge(s_k, 11)
                    eng.wait_ge(s_i, 48)
                ln_gains(name, eng)
                rotary_tables(name, eng, 0)
                stage_x(name, eng, 0, 0)
                front_x(name, eng, 0, 0)
                for c in range(6):
                    front_chunk(name, eng, 0, 0, c)
                for k in range(2):
                    for c in (2 * k, 2 * k + 1):
                        front_products(name, eng, 0, 0, c)
                        front_squares(name, eng, 0, 0, c)
                        front_sum(name, eng, 0, 0, c)
                    front_norms(name, eng, 0, 0, k)
                for c in range(4):
                    front_scale(name, eng, 0, 0, c)
                for t in range(TPB):
                    slot(name, eng, 0, t, with_ffn=False, first=(t == 0))
                with eng.Fori(0, STEPS - 2) as i:
                    for t in range(TPB):
                        slot(name, eng, 1 + i, t)
                for t in range(TPB - 1):
                    slot(name, eng, STEPS - 1, t)
                slot(name, eng, STEPS - 1, TPB - 1, last=True)
                slot(name, eng, STEPS, 0, after=True)
                ffn_alone(name, eng, STEPS - 1)

            lst = sig("lst", 5, "dve")
            lve = sig("lve", 1, "dve")
            lrs = sig("lrs", 1, "pool")
            lx = sig("lx", 4, "dve")

            def ln2(name, eng, b):
                if name == "dve":
                    for t in range(TPB):
                        lst.inc(eng.bn_stats(stats[:, t, :], X[:, b * TPB + t, :]))
                    lst.wait(eng, b, TPB - 1)
                    settle(eng)
                    for t in range(TPB):
                        i = eng.bn_aggr(mv[:, t, :], stats[:, t, :])
                    lst.inc(i)
                    lst.wait(eng, b)
                    lrs.wait(eng, b - 1)
                    lve.inc(eng.tensor_scalar(veps[:, :], mv[:, :, 1], LN_EPS, None, ALU.add))
                    lrs.wait(eng, b)
                    for t in range(TPB):
                        xt = X[:, b * TPB + t, :]
                        lx.inc(eng.tensor_scalar(xt, xt, mv[:, t, 0:1], rstd[:, t:t + 1],
                                                 ALU.subtract, ALU.mult))
                if name == "pool":
                    lve.wait(eng, b)
                    lx.wait(eng, b - 1)
                    lrs.inc(eng.tensor_tensor(rstd[:, :], veps[:, :], mhalf[:, 0:TPB], ALU.pow))

            engines_run(nc, sigs, layers_program)

        with ExitStack() as ctx:
            s_o = ctx.enter_context(nc.semaphore("s_o"))
            s_d = ctx.enter_context(nc.semaphore("s_d"))

            def out_program(name, eng):
                for b in range(BATCH):
                    r = slice(b * TPB, (b + 1) * TPB)
                    if name == "dve":
                        eng.tensor_tensor(XM[:, r, :], XM[:, r, :], X[:, r, :], ALU.add).then_inc(s_o, 1)
                    if name == "sp":
                        eng.wait_ge(s_o, b + 1)
                        eng.dma_start(out_t[:, r, :], XM[:, r, :]).then_inc(s_d, 16)
                if name == "sp":
                    eng.wait_ge(s_d, 16 * BATCH)

            engines_run(nc, (), out_program)


_INS = ['L0_attn_x', 'L0_attn_Wq', 'L0_attn_Wk', 'L0_attn_Wv', 'L0_attn_Wr', 'L0_ffn_Wqkv', 'L0_ffn_q_scale',
        'L0_ffn_k_scale', 'L0_ffn_Wo', 'L0_ffn_ln_g', 'L0_ffn_ln_b', 'L0_ffn_W1', 'L0_ffn_b1', 'L0_ffn_W2',
        'L0_ffn_b2']


def rotary_constants():
    import numpy as np
    f = np.float32
    half = np.arange(0, DH, 2, dtype=f)
    inv_freq = (f(1.0) / np.power(f(10000.0), half / f(DH))).astype(f)
    pos = np.arange(SEQ, dtype=f)
    freqs = (pos[:, None] * inv_freq[None, :]).astype(f)
    freqs = np.concatenate([freqs, freqs], -1).astype(np.float64)
    base = ((half + f(0.4 * DH)) / f(1.4 * DH)).astype(f)
    power = ((pos - SEQ // 2) / f(WIN // 2)).astype(f)
    scale = np.power(base[None, :].astype(np.float64), power[:, None])
    scale = np.concatenate([scale, scale], -1)
    sign = np.where(np.arange(DH) < DH // 2, -1.0, 1.0)
    cos, sin = np.cos(freqs), np.sin(freqs) * sign
    return np.stack([cos * scale * QK_SCALE, sin * scale * QK_SCALE, cos / scale, sin / scale]).astype(f)


def kernel(**inputs):
    import numpy as _np
    import concourse.bacc as _bacc
    from concourse import mybir as _mybir
    from concourse.bass_utils import run_bass_kernel_spmd as _run

    nc = _bacc.Bacc("TRN2", target_bir_lowering=False, num_devices=1)
    arrays, args = {}, []
    for name in _INS:
        arrays[f"in_{name}_dram"] = _np.ascontiguousarray(inputs[name])
    arrays["rotary_dram"] = rotary_constants()
    for name, a in arrays.items():
        args.append(nc.dram_tensor(name, a.shape, _mybir.dt.from_np(a.dtype), kind="ExternalInput").ap())
    args.append(nc.dram_tensor("out_0_dram", (BATCH, SEQ, E), F32, kind="ExternalOutput").ap())
    build(nc, *args)
    r = _run(nc, [arrays], core_ids=[0])
    return r.results[0]["out_0_dram"]
```
